# Optimizing a Trainium2 kernel written in Bass

```python
import numpy as np
import jax
import jax.numpy as jnp

def _softmax(x, axis=-1):
    return jax.nn.softmax(x, axis=axis)

def _gelu(x):
    return jax.nn.gelu(x, approximate=True)

def _silu(x):
    return jax.nn.silu(x)

def _sigmoid(x):
    return jax.nn.sigmoid(x)

def _layernorm(x, axis=-1, eps=1e-05):
    m = jnp.mean(x, axis=axis, keepdims=True)
    v = jnp.var(x, axis=axis, keepdims=True)
    return (x - m) / jnp.sqrt(v + eps)

def _scatter_add(tgt, idx, src, axis=0):
    return tgt.at[idx].add(src)

def _segment_sum(src, seg, n):
    return jax.ops.segment_sum(src, seg, n)
kernel_name = 'mk_seq_preln_d1_jaxref_r8_21e3c1'

def setup_inputs(seed: int=0):
    np.random.seed(seed)
    _w = jnp.asarray

    def _L0_attn_setup():
        import jax, jax.numpy as jnp
        import numpy as np
        B, S, D, H = (2, 256, 128, 16)
        DK = D // H
        key = jax.random.key(seed)
        ks = jax.random.split(key, 9)
        s = 0.02
        return {'embeddings': jax.random.normal(ks[0], (B, S, D), jnp.float32), 'Wq': jax.random.normal(ks[1], (H, D, DK), jnp.float32) * s, 'bq': jax.random.normal(ks[2], (H, DK), jnp.float32) * s, 'Wk': jax.random.normal(ks[3], (H, D, DK), jnp.float32) * s, 'bk': jax.random.normal(ks[4], (H, DK), jnp.float32) * s, 'Wv': jax.random.normal(ks[5], (H, D, DK), jnp.float32) * s, 'bv': jax.random.normal(ks[6], (H, DK), jnp.float32) * s, 'Wo': jax.random.normal(ks[7], (D, D), jnp.float32) * s, 'bo': jax.random.normal(ks[8], (D,), jnp.float32) * s}
    _L0_attn_in = _L0_attn_setup()

    def _L0_ffn_setup():
        import jax, jax.numpy as jnp
        import numpy as np
        B, S, D, H, M, E, K = (8, 256, 128, 256, 64, 8, 2)
        EH = H // 2

        def _layernorm(x, g, b, eps=1e-05):
            mu = jnp.mean(x, axis=-1, keepdims=True)
            var = jnp.var(x, axis=-1, keepdims=True)
            return (x - mu) * jax.lax.rsqrt(var + eps) * g + b
        key = jax.random.key(seed)
        ks = jax.random.split(key, 16)
        sc = lambda *shape: 1.0 / np.sqrt(shape[0])
        return {'inputs_embeds': jax.random.normal(ks[0], (B, S, D), jnp.float32), 'W_enc': jax.random.normal(ks[1], (D, H), jnp.float32) * sc(D), 'b_enc': jnp.zeros((H,), jnp.float32), 'W_s2c': jax.random.normal(ks[2], (H, M), jnp.float32) * sc(H), 'b_s2c': jnp.zeros((M,), jnp.float32), 'Wr': jax.random.normal(ks[3], (M, E), jnp.float32) * sc(M), 'br': jnp.zeros((E,), jnp.float32), 'W1': jax.random.normal(ks[4], (E, M, EH), jnp.float32) * sc(M), 'b1': jnp.zeros((E, EH), jnp.float32), 'W2': jax.random.normal(ks[5], (E, EH, M), jnp.float32) * sc(EH), 'b2': jnp.zeros((E, M), jnp.float32), 'W_c2s': jax.random.normal(ks[6], (M, H), jnp.float32) * sc(M), 'b_c2s': jnp.zeros((H,), jnp.float32), 'W_dec': jax.random.normal(ks[7], (H, D), jnp.float32) * sc(H), 'b_dec': jnp.zeros((D,), jnp.float32), 'ln_g': jnp.ones((D,), jnp.float32), 'ln_b': jnp.zeros((D,), jnp.float32)}
    _L0_ffn_in = _L0_ffn_setup()
    _d = {'L0_attn_embeddings': _L0_attn_in['embeddings'], 'L0_attn_Wq': _L0_attn_in['Wq'], 'L0_attn_bq': _L0_attn_in['bq'], 'L0_attn_Wk': _L0_attn_in['Wk'], 'L0_attn_bk': _L0_attn_in['bk'], 'L0_attn_Wv': _L0_attn_in['Wv'], 'L0_attn_bv': _L0_attn_in['bv'], 'L0_attn_Wo': _L0_attn_in['Wo'], 'L0_attn_bo': _L0_attn_in['bo'], 'L0_ffn_W_enc': _L0_ffn_in['W_enc'], 'L0_ffn_b_enc': _L0_ffn_in['b_enc'], 'L0_ffn_W_s2c': _L0_ffn_in['W_s2c'], 'L0_ffn_b_s2c': _L0_ffn_in['b_s2c'], 'L0_ffn_Wr': _L0_ffn_in['Wr'], 'L0_ffn_br': _L0_ffn_in['br'], 'L0_ffn_W1': _L0_ffn_in['W1'], 'L0_ffn_b1': _L0_ffn_in['b1'], 'L0_ffn_W2': _L0_ffn_in['W2'], 'L0_ffn_b2': _L0_ffn_in['b2'], 'L0_ffn_W_c2s': _L0_ffn_in['W_c2s'], 'L0_ffn_b_c2s': _L0_ffn_in['b_c2s'], 'L0_ffn_W_dec': _L0_ffn_in['W_dec'], 'L0_ffn_b_dec': _L0_ffn_in['b_dec'], 'L0_ffn_ln_g': _L0_ffn_in['ln_g'], 'L0_ffn_ln_b': _L0_ffn_in['ln_b']}
    _x0 = _d['L0_attn_embeddings']
    _d['L0_attn_embeddings'] = jax.random.normal(jax.random.fold_in(jax.random.key(seed), 1), (4, 512, 128), dtype=_x0.dtype)
    del _x0
    return _d

def reference(L0_attn_embeddings, L0_attn_Wq, L0_attn_bq, L0_attn_Wk, L0_attn_bk, L0_attn_Wv, L0_attn_bv, L0_attn_Wo, L0_attn_bo, L0_ffn_W_enc, L0_ffn_b_enc, L0_ffn_W_s2c, L0_ffn_b_s2c, L0_ffn_Wr, L0_ffn_br, L0_ffn_W1, L0_ffn_b1, L0_ffn_W2, L0_ffn_b2, L0_ffn_W_c2s, L0_ffn_b_c2s, L0_ffn_W_dec, L0_ffn_b_dec, L0_ffn_ln_g, L0_ffn_ln_b):

    def _L0_attn_ref(embeddings, Wq, bq, Wk, bk, Wv, bv, Wo, bo):
        import jax, jax.numpy as jnp
        import numpy as np
        B, S, D, H = (2, 256, 128, 16)
        DK = D // H
        b, s, d = embeddings.shape
        dk = Wq.shape[-1]
        q = jnp.einsum('bsd,hdk->bhsk', embeddings, Wq) + bq[None, :, None, :]
        k = jnp.einsum('bsd,hdk->bhsk', embeddings, Wk) + bk[None, :, None, :]
        v = jnp.einsum('bsd,hdk->bhsk', embeddings, Wv) + bv[None, :, None, :]
        scores = jnp.einsum('bhqk,bhsk->bhqs', q, k) / jnp.sqrt(jnp.float32(dk))
        causal_mask = jnp.triu(jnp.ones((s, s), dtype=bool), k=1)
        scores = jnp.where(causal_mask, jnp.float32(-1000000000.0), scores)
        weights = jax.nn.softmax(scores, axis=-1)
        ctx = jnp.einsum('bhqs,bhsk->bhqk', weights, v)
        concat = ctx.transpose(0, 2, 1, 3).reshape(b, s, d)
        return concat @ Wo + bo

    def _L0_ffn_ref(inputs_embeds, W_enc, b_enc, W_s2c, b_s2c, Wr, br, W1, b1, W2, b2, W_c2s, b_c2s, W_dec, b_dec, ln_g, ln_b):
        import jax, jax.numpy as jnp
        import numpy as np
        B, S, D, H, M, E, K = (8, 256, 128, 256, 64, 8, 2)
        EH = H // 2

        def _layernorm(x, g, b, eps=1e-05):
            mu = jnp.mean(x, axis=-1, keepdims=True)
            var = jnp.var(x, axis=-1, keepdims=True)
            return (x - mu) * jax.lax.rsqrt(var + eps) * g + b
        b, s, d = inputs_embeds.shape
        spikes_enc = jax.nn.sigmoid(inputs_embeds @ W_enc + b_enc)
        flat = spikes_enc.reshape(b * s, -1)
        cont = flat @ W_s2c + b_s2c
        probs = jax.nn.softmax(cont @ Wr + br, axis=-1)
        topk_w, topk_idx = jax.lax.top_k(probs, K)
        topk_w = topk_w / jnp.sum(topk_w, axis=-1, keepdims=True)
        gate = jnp.sum(jax.nn.one_hot(topk_idx, E, dtype=cont.dtype) * topk_w[..., None], axis=1)
        h = jax.nn.relu(jnp.einsum('tm,emh->eth', cont, W1) + b1[:, None, :])
        y = jnp.einsum('eth,ehm->etm', h, W2) + b2[:, None, :]
        expert_out = jnp.einsum('etm,te->tm', y, gate)
        spikes_moe = jax.nn.sigmoid(expert_out @ W_c2s + b_c2s)
        spikes_moe = spikes_moe.reshape(b, s, -1)
        decoded = spikes_moe @ W_dec + b_dec
        return _layernorm(decoded, ln_g, ln_b)
    x = L0_attn_embeddings
    x = x + _L0_attn_ref(_layernorm(x, axis=-1), L0_attn_Wq, L0_attn_bq, L0_attn_Wk, L0_attn_bk, L0_attn_Wv, L0_attn_bv, L0_attn_Wo, L0_attn_bo)
    x = x + _L0_ffn_ref(_layernorm(x, axis=-1), L0_ffn_W_enc, L0_ffn_b_enc, L0_ffn_W_s2c, L0_ffn_b_s2c, L0_ffn_Wr, L0_ffn_br, L0_ffn_W1, L0_ffn_b1, L0_ffn_W2, L0_ffn_b2, L0_ffn_W_c2s, L0_ffn_b_c2s, L0_ffn_W_dec, L0_ffn_b_dec, L0_ffn_ln_g, L0_ffn_ln_b)
    return x

_drawn_inputs = setup_inputs


def setup_inputs(seed=0):
    import zlib

    import numpy as np

    out = dict(_drawn_inputs(seed))
    spreads = {'L0_ffn_b_enc': (0.0, 0.556),
     'L0_ffn_b_s2c': (0.0, 0.1),
     'L0_ffn_br': (0.0, 0.1),
     'L0_ffn_b1': (0.0, 0.518),
     'L0_ffn_b2': (0.0, 0.389),
     'L0_ffn_b_c2s': (0.0, 0.347),
     'L0_ffn_b_dec': (0.0, 0.1),
     'L0_ffn_ln_g': (1.0, 0.2),
     'L0_ffn_ln_b': (0.0, 0.1)}
    factors = {'L0_attn_Wq': 8.0,
     'L0_attn_bq': 8.0,
     'L0_attn_Wk': 8.0,
     'L0_attn_bk': 64.0,
     'L0_attn_Wv': 8.0,
     'L0_attn_bv': 8.0,
     'L0_attn_Wo': 8.0,
     'L0_attn_bo': 3.629}
    for name, (base, spread) in spreads.items():
        noise = np.random.default_rng([zlib.crc32(name.encode()), seed]).standard_normal(out[name].shape)
        drawn = base * np.exp(spread * noise) if base else spread * noise
        out[name] = jnp.asarray(drawn.astype(out[name].dtype))
    for name, factor in factors.items():
        out[name] = (out[name] * factor).astype(out[name].dtype)
    return out
```

```python
from contextlib import ExitStack

import concourse.bass as bass
from concourse import mybir

ALU = mybir.AluOpType
ACT = mybir.ActivationFunctionType
F32 = mybir.dt.float32
BF16 = mybir.dt.bfloat16
AX_X = mybir.AxisListType.X

P = 128
EPS = 1e-5
MASKED = -1e30
PARTS = 3
M_ROW = 96


def split_rows(i, j, d):
    r = (PARTS * i + j) * d
    return r, r + d


def max_units(tiles, group):
    units = []
    for t in reversed(range(tiles)):
        n = max(1, tiles // (t + 1)) if (t + 1) * group > tiles else group
        n = min(n, group)
        units += [(t, h, n) for h in range(0, group, n)]
    return units


def schedule(B, groups, n_max, n_score, n_pv):
    yield ("norm1", 0)
    for what in ("xT", "q", "k", "v"):
        yield (what, 0)
    yield ("ffn_setup",)
    for n in range(groups * n_max):
        yield ("max", 0, n)
    yield ("negmax", 0)
    for b in range(B):
        nb = b + 1
        ahead = iter(range(groups * n_max if nb < B else 0))

        def maxima(count):
            for _ in range(count):
                n = next(ahead, None)
                if n is not None:
                    yield ("max", nb, n)

        for g in range(groups):
            for u in range(n_score):
                yield ("score", b, g, u)
                if g and u in (3, 5, 7, 8):
                    yield ("pv", b, g - 1, (3, 5, 7, 8).index(u))
                if g == 0 and nb < B:
                    if u == 0:
                        yield ("norm1", nb)
                    if u in (3, 5, 6, 7):
                        yield (("xT", "q", "k", "v")[(3, 5, 6, 7).index(u)], nb)
                if g == 2 and u == 9:
                    yield ("ctx_out", b, 0)
                if g == 3 and u == 3:
                    yield ("ctx_tok", b, 0)
                if g:
                    yield from maxima(1)
        for c in range(n_pv):
            yield ("pv", b, groups - 1, c)
            yield from maxima(1)
        yield ("ctx_out", b, 1)
        yield from maxima(2)
        yield ("ctx_tok", b, 1)
        yield from maxima(2)
        yield ("ctxT", b)
        yield from maxima(1)
        yield ("out_proj", b)
        yield ("norm2", b)
        yield from maxima(6)
        yield ("x1T", b)
        yield from maxima(1)
        yield ("enc", b, 0)
        yield ("enc", b, 1)
        yield from maxima(1)
        yield ("s2c", b)
        yield from maxima(99)
        yield ("router", b)
        for e in range(8):
            yield ("w1", b, e)
            if e == 4 and nb < B:
                yield ("negmax", nb)
        yield ("gateT", b)
        for e in range(8):
            yield ("gate", b, e)
            if e >= 1:
                yield ("w2", b, e - 1)
        yield ("w2", b, 7)
        yield ("c2s", b, 0)
        yield ("c2s", b, 1)
        yield ("dec", b)


def build(nc, a, out):
    B, S, D = a["L0_attn_embeddings"].shape
    H, _, DK = a["L0_attn_Wq"].shape
    HID = a["L0_ffn_W_enc"].shape[1]
    M = a["L0_ffn_W_s2c"].shape[1]
    E, _, EH = a["L0_ffn_W1"].shape
    T = S // P
    HC = HID // P
    GH = 4
    G = H // GH
    NS = 10
    SLOTS = 16
    NPV = 4
    QSCALE = float(DK) ** -0.5
    VW = 32
    SLOT = DK + 1
    assert (D, EH, S, H * DK, 2 * M, GH) == (P, P, 512, P, P, T)

    MU = []
    for g in range(G):
        MU += [(t, GH * g + h, n) for t, h, n in max_units(T, GH)]
    NM = len(MU) // G
    steps = list(schedule(B, G, NM, NS, NPV))

    ring_a = {s: n for n, s in enumerate([s for s in steps if s[0] in ("xT", "q", "k", "v", "max", "negmax")])}
    ring_m = {s: n for n, s in enumerate([s for s in steps if s[0] in (
        "ctx_tok", "ctxT", "out_proj", "x1T", "enc", "s2c", "router", "w1", "gateT", "gate", "c2s", "dec")])}

    with ExitStack() as ctx:
        def sb(name, shape, dt=F32):
            return ctx.enter_context(nc.sbuf_tensor(name, shape, dt))

        def sem(name):
            return ctx.enter_context(nc.semaphore(name))

        ps_a = [ctx.enter_context(nc.psum_tensor(f"ps_a{i}", [P, 512], F32)) for i in range(2)]
        ps_b = [ctx.enter_context(nc.psum_tensor(f"ps_b{i}", [P, 512], F32)) for i in range(2)]
        ps_v = [ctx.enter_context(nc.psum_tensor(f"ps_v{i}", [P, 512], F32)) for i in range(2)]
        ps_m = [ctx.enter_context(nc.psum_tensor(f"ps_m{i}", [P, 512], F32)) for i in range(2)]

        ident = sb("ident", [P, P])
        identb = sb("identb", [P, P], BF16)
        mask = sb("mask", [P, 4, P], BF16)
        ones = sb("ones", [P, P])
        minus_half = sb("minus_half", [P, T])
        tie_rank = sb("tie_rank", [P, T, E])
        sel = sb("sel", [96, E, P], BF16)
        x_all = sb("x_all", [P, B * T, D])
        w_qk_raw = sb("w_qk_raw", [P, 2, H, DK])
        w_qk = sb("w_qk", [P, 2, DK, H])
        wv = sb("wv", [P, H, DK])
        bq_raw = sb("bq_raw", [P, 1])
        bqs = sb("bqs", [P, 1])
        bk = sb("bk", [P, 1])
        bv = sb("bv", [P, T, H * DK])
        wo = sb("wo", [P, D])
        bo = sb("bo", [P, D])
        w_enc = sb("w_enc", [P, HID])
        b_enc = sb("b_enc", [P, HC])
        w_s2c = sb("w_s2c", [P, HC, M])
        b_s2c = sb("b_s2c", [P, 1])
        wr = sb("wr", [P, E])
        br = sb("br", [P, T, E])
        zeros_b = sb("zeros_b", [M_ROW - PARTS * PARTS * DK, S], BF16)
        ones_b = sb("ones_b", [PARTS, S], BF16)
        w1 = sb("w1", [P, E, EH])
        b1 = sb("b1", [P, E])
        w2 = sb("w2", [P, E, M])
        b2f = sb("b2f", [96, M])
        b2r = sb("b2r", [96, M])
        b2s = sb("b2s", [96, PARTS, M], BF16)
        w_c2s = sb("w_c2s", [P, HID])
        b_c2s = sb("b_c2s", [P, HC])
        w_dec = sb("w_dec", [P, HC, D])
        b_dec = sb("b_dec", [P, D])
        ln_g = sb("ln_g", [P, D])
        ln_b = sb("ln_b", [P, D])

        st1 = sb("st1", [P, T, 6])
        mv1 = sb("mv1", [P, T, 2])
        rs1 = sb("rs1", [P, T])
        xn = sb("xn", [P, T, D])
        xT = sb("xT", [P, S])
        qkf = sb("qkf", [P, 2, S])
        qkr = sb("qkr", [P, S])
        parts = sb("parts", [P, 2, PARTS, S], BF16)
        qs = [sb(f"qs{i}", [P, H, S], BF16) for i in range(2)]
        ks = [sb(f"ks{i}", [P, H, S], BF16) for i in range(2)]
        vp = [sb(f"vp{i}", [P, T, H, VW]) for i in range(2)]
        mx = sb("mx", [P, T, H])
        nmf = sb("nmf", [H, S])
        nmr = sb("nmr", [H, S])
        nmp = sb("nmp", [H, PARTS, S], BF16)
        pr = sb("pr", [P, SLOTS, S])
        cu = sb("cu", [P, 2, S])
        rsum = sb("rsum", [P, T, GH, 2])
        ctok = sb("ctok", [P, T, H * DK])
        dT = sb("dT", [P, S])

        x1 = sb("x1", [P, T, D])
        st2 = sb("st2", [P, T, 6])
        mv2 = sb("mv2", [P, T, 2])
        rs2 = sb("rs2", [P, T])
        xn2 = sb("xn2", [P, T, D])
        spikes = sb("spikes", [P, HC, S])
        cont = sb("cont", [P, S])
        lg = sb("lg", [P, T, E])
        ex = sb("ex", [P, T, E])
        ra = sb("ra", [P, T, E])
        rb = sb("rb", [P, T, E])
        oh1 = sb("oh1", [P, T, E])
        oh2 = sb("oh2", [P, T, E])
        r1 = sb("r1", [P, T])
        gate = sb("gate", [P, T, E])
        g2 = sb("g2", [E, S], BF16)
        gs = sb("gs", [96, S], BF16)
        hs = sb("hs", [P, E, S])
        z = sb("z", [P, T, D])
        st3 = sb("st3", [P, T, 6])
        mv3 = sb("mv3", [P, T, 2])
        rs3 = sb("rs3", [P, T])

        x_in = [sem(f"x_in{b}") for b in range(B)]
        qkv_in = sem("qkv_in")
        ffn_in = sem("ffn_in")
        filled = sem("filled")
        consts = sem("consts")
        vp_ones = sem("vp_ones")
        rows_set = [sem(f"rows_set{i}") for i in range(2)]
        ones_ready = sem("ones_ready")
        bias_in = sem("bias_in")
        bqs_ready = sem("bqs_ready")
        w_turned = sem("w_turned")
        halved = sem("halved")
        b2_split = sem("b2_split")
        sums_ps = sem("sums_ps")
        biases = sem("biases")
        a_filled = [sem(f"a_filled{i}") for i in range(2)]
        a_freed = [sem(f"a_freed{i}") for i in range(2)]
        m_filled = [sem(f"m_filled{i}") for i in range(2)]
        m_freed = [sem(f"m_freed{i}") for i in range(2)]
        ln1 = sem("ln1")
        rstd1 = sem("rstd1")
        xn_ready = sem("xn_ready")
        x_bo = sem("x_bo")
        qk_split = sem("qk_split")
        stacked = [sem(f"stacked{i}") for i in range(2)]
        nm_split = sem("nm_split")
        nm_in = [sem(f"nm_in{i}") for i in range(2)]
        scores = sem("scores")
        probs = sem("probs")
        masked = sem("masked")
        pv_done = sem("pv_done")
        ctx_sb = sem("ctx_sb")
        recip = sem("recip")
        ln2 = sem("ln2")
        rstd2 = sem("rstd2")
        xn2_ready = sem("xn2_ready")
        x1_lnb = sem("x1_lnb")
        routed = sem("routed")
        route_exp = sem("route_exp")
        gate_split = sem("gate_split")
        y_filled = sem("y_filled")
        y_ready = sem("y_ready")
        ln3 = sem("ln3")
        rstd3 = sem("rstd3")
        zn_ready = sem("zn_ready")
        zn_scaled = sem("zn_scaled")
        res_ready = sem("res_ready")
        stored = sem("stored")

        QKV_LOADS = 8
        FFN_LOADS = 27
        STACKS = 2 * PARTS * PARTS
        ROUTE = 18

        def bank(ring, s):
            n = ring[s]
            return n % 2, n // 2

        def take(eng, ring, freed, s):
            i, r = bank(ring, s)
            if r:
                eng.wait_ge(freed[i], r)
            return i

        def read(eng, ring, freed, s):
            i, r = bank(ring, s)
            eng.wait_ge(freed[i], r + 1)

        def full(eng, ring, filled, s):
            i, r = bank(ring, s)
            eng.wait_ge(filled[i], r + 1)
            return i

        def score_parts(u):
            if u < 4:
                return [(u, 0, 0)]
            if u < 8:
                return [(u - 4, 1, 0), (u - 4, 3, S - P)]
            return [(2 * (u - 8) + i, 2, i * 2 * P) for i in range(2)]

        def prob_slot(b, g, u):
            return ((b * G + g) * NS + u) % SLOTS

        def pv_count(n):
            return NPV * (n // NS) + (1, 3, 4)[n % NS // 4]

        block = ctx.enter_context(nc.Block())

        @block.sync
        def _(sp):
            x_dram = a["L0_attn_embeddings"].rearrange("b (t p) d -> p b t d", p=P)
            with nc.allow_non_contiguous_dma(reason="small transposed biases"):
                sp.dma_start(x_all[:, 0:T, :], x_dram[:, 0]).then_inc(x_in[0], 16)
                for dst, name in ((w_qk_raw[:, 0], "Wq"), (w_qk_raw[:, 1], "Wk"), (wv[:, :, :], "Wv")):
                    sp.dma_start(dst, a[f"L0_attn_{name}"].rearrange("h d k -> d h k")).then_inc(qkv_in, 16)
                for dst, name in ((bq_raw, "bq"), (bk, "bk")):
                    for k in range(DK):
                        sp.dma_start(dst[H * k:H * k + H, :], a[f"L0_attn_{name}"][:, k:k + 1]).then_inc(bias_in, 16)
                flat = a["L0_attn_bv"].rearrange("h k -> (h k)")
                for t in range(T):
                    sp.dma_start(bv[:, t, :], flat.partition_broadcast(P)).then_inc(qkv_in, 16)
                sp.dma_start(bo[:, :], a["L0_attn_bo"].partition_broadcast(P)).then_inc(qkv_in, 16)
                sp.wait_ge(filled, 2)
                r0 = PARTS * PARTS * DK
                for i in range(2):
                    for st in (qs[i], ks[i]):
                        sp.dma_start(st[r0:M_ROW, :, :], zeros_b[:, :].unsqueeze(1).to_broadcast([M_ROW - r0, H, S])
                                     ).then_inc(rows_set[i], 16)
                    sp.dma_start(ks[i][M_ROW:M_ROW + PARTS, :, :],
                                 ones_b[:, :].unsqueeze(1).to_broadcast([PARTS, H, S])).then_inc(rows_set[i], 16)
                for b in range(1, B):
                    sp.dma_start(x_all[:, T * b:T * b + T, :], x_dram[:, b]).then_inc(x_in[b], 16)

            for s in steps:
                if s[0] in ("q", "k"):
                    b, which = s[1], int(s[0] == "k")
                    dst = (ks if which else qs)[b % 2]
                    if b >= 2:
                        sp.wait_ge(pv_done, NPV * G * (b - 1))
                    for part in range(PARTS):
                        sp.wait_ge(qk_split, 8 * b + 4 * which + (1, 3, 4)[part])
                        for other in range(PARTS):
                            r0, r1_ = split_rows(other, part, DK) if which else split_rows(part, other, DK)
                            sp.dma_start(dst[r0:r1_, :, :], parts[:, which, part, :]).then_inc(stacked[b % 2], 16)
                if s[0] == "negmax":
                    b = s[1]
                    for part in range(PARTS):
                        sp.wait_ge(nm_split, 4 * b + (1, 3, 4)[part])
                        sp.dma_start(qs[b % 2][M_ROW + part:M_ROW + part + 1, :, :],
                                     nmp[:, part, :]).then_inc(nm_in[b % 2], 16)
                if s[0] == "dec":
                    b = s[1]
                    sp.wait_ge(res_ready, b + 1)
                    sp.dma_start(out.rearrange("b (t p) d -> p b t d", p=P)[:, b], z[:, :, :]).then_inc(stored, 16)
            sp.wait_ge(stored, 16 * B)

        @block.gpsimd
        def _(pool):
            nc.gpsimd.memset(zeros_b[:, :], 0.0).then_inc(filled, 1)
            nc.gpsimd.memset(ones_b[:, :], 1.0).then_inc(filled, 1)
            nc.gpsimd.memset(b2f[:, :], 0.0).then_inc(filled, 1)
            nc.gpsimd.memset(b_s2c[:, :], 0.0).then_inc(filled, 1)
            for t_ in (ident, identb, mask):
                nc.gpsimd.memset(t_[:], 0.0).then_inc(filled, 1)
            nc.gpsimd.memset(minus_half[:, :], -0.5).then_inc(filled, 1)
            pool.wait_ge(filled, 8)
            nc.gpsimd.affine_select(out=ident[:, :], in_=ident[:, :], compare_op=ALU.not_equal, fill=1.0, base=0,
                                    pattern=[[-1, P]], channel_multiplier=1).then_inc(consts, 1)

            def other_constants():
                nc.gpsimd.affine_select(out=identb[:, :], in_=identb[:, :], compare_op=ALU.not_equal, fill=1.0,
                                        base=0, pattern=[[-1, P]], channel_multiplier=1).then_inc(consts, 1)
                nc.gpsimd.affine_select(out=mask[:, :, :], in_=mask[:, :, :], compare_op=ALU.is_ge, fill=MASKED,
                                        base=0, pattern=[[0, 4], [-1, P]], channel_multiplier=1).then_inc(consts, 1)
                for n in range(2):
                    nc.gpsimd.memset(vp[n][:, :, :, :], 0.0).then_inc(filled, 1)
                pool.wait_ge(filled, 10)
                for n in range(2):
                    for second in range(2):
                        v = vp[n][:, :, :, :].rearrange("p t (a h) w -> p (t a) h w", h=2 * GH)
                        c = SLOT * second + DK
                        nc.gpsimd.memset(v[:, :, GH * second:GH * second + GH, c:c + 1], 1.0).then_inc(vp_ones, 1)
                nc.gpsimd.memset(sel[:, :, :], 0.0).then_inc(filled, 1)
                pool.wait_ge(filled, 11)
                for i in range(PARTS):
                    v = sel[32 * i:32 * i + 32, :, :]
                    nc.gpsimd.affine_select(out=v, in_=v, compare_op=ALU.not_equal, fill=1.0, base=0,
                                            pattern=[[-1, E], [0, P]], channel_multiplier=1).then_inc(consts, 1)
                    pool.wait_ge(consts, 4 + i)
                for e in range(E):
                    nc.gpsimd.memset(tie_rank[:, :, e:e + 1], float(E - e)).then_inc(consts, 1)

            for s in steps:
                kind, b = s[0], (s[1] if len(s) > 1 else 0)
                if kind in ("norm1", "norm2", "dec"):
                    stats, rstd, mv, rs = {"norm1": (ln1, rstd1, mv1, rs1), "norm2": (ln2, rstd2, mv2, rs2),
                                           "dec": (ln3, rstd3, mv3, rs3)}[kind]
                    pool.wait_ge(stats, 2 * T * (b + 1))
                    nc.gpsimd.tensor_scalar(rs[:, :], mv[:, :, 1], EPS, None, ALU.add).then_inc(rstd, 1)
                    pool.wait_ge(rstd, 2 * b + 1)
                    nc.gpsimd.tensor_tensor(rs[:, :], rs[:, :], minus_half[:, :], ALU.pow).then_inc(rstd, 1)
                if kind == "norm1" and b == 0:
                    other_constants()
                if kind == "v":
                    pool.wait_ge(xn_ready, T * (b + 1))
                    pool.wait_ge(qkv_in, 16 * QKV_LOADS)
                    xb = x_all[:, T * b:T * b + T, :]
                    nc.gpsimd.tensor_tensor(xb, xb, bo[:, :].unsqueeze(1).to_broadcast([P, T, D]),
                                            ALU.add).then_inc(x_bo, 1)
                if kind == "score":
                    _, _, g, u = s
                    slot = pr[:, prob_slot(b, g, u), :]
                    pool.wait_ge(probs, (b * G + g) * NS + u + 1)
                    if u < 4:
                        n, v = 1, slot[:, 0:P].rearrange("p (a c) -> p a c", a=1)
                    elif u < 8:
                        n, v = 2, slot.rearrange("p (a c) -> p a c", c=P)[:, 0:4:3, :]
                    else:
                        n, v = 2, slot.rearrange("p (a c) -> p a c", a=2)[:, :, 0:P]
                    nc.gpsimd.affine_select(out=v, in_=v, compare_op=ALU.is_ge, fill=0.0, base=0,
                                            pattern=[[0, n], [1, P]], channel_multiplier=-1).then_inc(masked, 1)
                if kind == "norm2":
                    pool.wait_ge(ffn_in, 16 * FFN_LOADS)
                    nc.gpsimd.tensor_tensor(x_all[:, T * b:T * b + T, :], x1[:, :, :], ln_b[:, :].unsqueeze(1).to_broadcast([P, T, D]),
                                            ALU.add).then_inc(x1_lnb, 1)
                if kind == "dec":
                    pool.wait_ge(zn_ready, T * (b + 1))
                    nc.gpsimd.tensor_tensor(xn2[:, :, :], xn2[:, :, :], ln_g[:, :].unsqueeze(1).to_broadcast([P, T, D]),
                                            ALU.mult).then_inc(zn_scaled, 1)

        @block.scalar
        def _(act):
            with nc.allow_non_contiguous_dma(reason="small transposed biases"):
                def load(dst, src):
                    act.dma_start(dst, src).then_inc(ffn_in, 16)
                act.wait_ge(filled, 4)
                load(wo[:, :], a["L0_attn_Wo"])
                load(w_enc[:, :], a["L0_ffn_W_enc"])
                for c in range(HC):
                    load(b_enc[:, c:c + 1], a["L0_ffn_b_enc"][P * c:P * c + P].unsqueeze(1))
                    load(b_c2s[:, c:c + 1], a["L0_ffn_b_c2s"][P * c:P * c + P].unsqueeze(1))
                load(w_s2c[:, :, :], a["L0_ffn_W_s2c"].rearrange("(c p) m -> p c m", p=P))
                load(b_s2c[0:M, :], a["L0_ffn_b_s2c"].unsqueeze(1))
                for i in range(2):
                    load(wr[M * i:M * i + M, :], a["L0_ffn_Wr"])
                    load(w1[M * i:M * i + M, :, :], a["L0_ffn_W1"].rearrange("e m h -> m e h"))
                    load(w_c2s[M * i:M * i + M, :], a["L0_ffn_W_c2s"])
                for t in range(T):
                    act.dma_start(br[:, t, :], a["L0_ffn_br"].partition_broadcast(P)).then_inc(ffn_in, 16)
                load(b1[:, :], a["L0_ffn_b1"].rearrange("e h -> h e"))
                load(w2[:, :, :], a["L0_ffn_W2"].rearrange("e h m -> h e m"))
                for i in range(PARTS):
                    act.dma_start(b2f[32 * i:32 * i + E, :], a["L0_ffn_b2"]).then_inc(ffn_in, 16)
                load(w_dec[:, :, :], a["L0_ffn_W_dec"].rearrange("(c p) d -> p c d", p=P))
                load(b_dec[:, :], a["L0_ffn_b_dec"].partition_broadcast(P))
                load(ln_g[:, :], a["L0_ffn_ln_g"].partition_broadcast(P))
                load(ln_b[:, :], a["L0_ffn_ln_b"].partition_broadcast(P))

            act.wait_ge(qkv_in, 16 * QKV_LOADS)
            nc.scalar.copy(w_qk[:, :, :, :], w_qk_raw[:, :, :, :].rearrange("p w h k -> p w k h")).then_inc(w_turned, 1)

            for s in steps:
                kind, b = s[0], (s[1] if len(s) > 1 else 0)
                if kind == "xT":
                    i = full(act, ring_a, a_filled, s)
                    if b:
                        j, r = bank(ring_a, ("v", b - 1))
                        act.wait_ge(a_filled[j], r + 1)
                    nc.scalar.copy(xT[:, :], ps_a[i][:, :]).then_inc(a_freed[i], 1)
                if kind == "q":
                    i = full(act, ring_a, a_filled, s)
                    act.wait_ge(bqs_ready, 1)
                    if b:
                        act.wait_ge(qk_split, 8 * b)
                    nc.scalar.activation(qkf[:, 0, :], ps_a[i][:, :], ACT.Identity, bias=bqs[:, 0:1],
                                         scale=QSCALE).then_inc(a_freed[i], 1)
                if kind == "k":
                    i = full(act, ring_a, a_filled, s)
                    nc.scalar.activation(qkf[:, 1, :], ps_a[i][:, :], ACT.Identity,
                                         bias=bk[:, 0:1]).then_inc(a_freed[i], 1)
                if kind == "score":
                    _, _, g, u = s
                    n = (b * G + g) * NS + u
                    act.wait_ge(scores, n + 1)
                    if n >= SLOTS:
                        act.wait_ge(pv_done, pv_count(n - SLOTS))
                    nc.scalar.activation(pr[:, prob_slot(b, g, u), :], ps_b[n % 2][:, :],
                                         ACT.Exp).then_inc(probs, 1)
                if kind == "ctx_out":
                    half = s[2]
                    act.wait_ge(pv_done, NPV * (b * G + 2 * (half + 1)))
                    if b:
                        j, r = bank(ring_m, ("ctx_tok", b - 1, half))
                        act.wait_ge(m_filled[j], r + 1)
                    nc.scalar.copy(cu[:, half, :], ps_v[half][:, :]).then_inc(ctx_sb, 1)
                if kind in ("ctxT", "x1T"):
                    i = full(act, ring_m, m_filled, s)
                    nc.scalar.copy(dT[:, :], ps_m[i][:, :]).then_inc(m_freed[i], 1)
                if kind in ("enc", "c2s"):
                    c = s[2]
                    if b == 0 and c == 0:
                        act.wait_ge(biases, 2)
                    i = full(act, ring_m, m_filled, s)
                    bias = b_enc if kind == "enc" else b_c2s
                    nc.scalar.activation(spikes[:, c, :], ps_m[i][:, :], ACT.Tanh, bias=bias[:, c:c + 1],
                                         scale=0.5).then_inc(m_freed[i], 1)
                if kind == "s2c":
                    i = full(act, ring_m, m_filled, s)
                    nc.scalar.activation(cont[:, :], ps_m[i][:, :], ACT.Identity,
                                         bias=b_s2c[:, 0:1]).then_inc(m_freed[i], 1)
                if kind == "w1":
                    e = s[2]
                    i = full(act, ring_m, m_filled, s)
                    nc.scalar.activation(hs[:, e, :], ps_m[i][:, :], ACT.Relu,
                                         bias=b1[:, e:e + 1]).then_inc(m_freed[i], 1)
                    if e == 1:
                        act.wait_ge(routed, ROUTE * b + 2)
                        nc.scalar.activation(ex[:, :, :], lg[:, :, :], ACT.Exp).then_inc(route_exp, 1)
                if kind == "w2" and s[2] == E - 1:
                    act.wait_ge(y_filled, b + 1)
                    nc.scalar.copy(cont[:, :], ps_v[0][:, :]).then_inc(y_ready, 1)

        @block.tensor
        def _(pe):
            def mm(*args, start=True, stop=True):
                return nc.tensor.matmul(*args, start=start, stop=stop)

            def turn(dst, src):
                return nc.tensor.transpose(dst, src, ident[0:src.shape[0], 0:src.shape[0]])

            for s in steps:
                kind, b = s[0], (s[1] if len(s) > 1 else 0)
                if kind == "ffn_setup":
                    pe.wait_ge(consts, 3 + PARTS + E)
                    pe.wait_ge(ones_ready, 2)
                    pe.wait_ge(halved, 4)
                    for c in range(HC):
                        mm(ps_m[0][0:M, 0:1], w_s2c[:, c, :], ones[:, 0:1], start=(c == 0), stop=(c == HC - 1))
                    for c in range(HC):
                        last = mm(ps_v[0][:, 0:D], ones[:, :], w_dec[:, c, :], start=(c == 0), stop=(c == HC - 1))
                    last.then_inc(sums_ps, 1)
                if kind == "xT":
                    i = take(pe, ring_a, a_freed, s)
                    if b == 0:
                        pe.wait_ge(consts, 1)
                    pe.wait_ge(xn_ready, T * (b + 1))
                    for t in range(T):
                        last = turn(ps_a[i][:, P * t:P * t + P], xn[:, t, :])
                    last.then_inc(a_filled[i], 1)
                if kind in ("q", "k"):
                    i = take(pe, ring_a, a_freed, s)
                    if kind == "q":
                        read(pe, ring_a, a_freed, ("xT", b))
                        pe.wait_ge(w_turned, 1)
                    w = w_qk[:, int(kind == "k")].rearrange("p k h -> p (k h)")
                    mm(ps_a[i][:, :], w, xT[:, :]).then_inc(a_filled[i], 1)
                if kind == "v":
                    i = take(pe, ring_a, a_freed, s)
                    for t in range(T):
                        last = mm(ps_a[i][:, P * t:P * t + P], xT[:, P * t:P * t + P],
                                  wv[:, :, :].rearrange("p h k -> p (h k)"))
                    last.then_inc(a_filled[i], 1)
                if kind == "max":
                    t, h0, nh = MU[s[2]]
                    i = take(pe, ring_a, a_freed, s)
                    if s[2] == 0:
                        pe.wait_ge(stacked[b % 2], 16 * STACKS * (b // 2 + 1))
                        pe.wait_ge(rows_set[b % 2], 16 * 3)
                    W = P * (t + 1)
                    for n in range(nh):
                        mm(ps_a[i][:, n * W:n * W + W], qs[b % 2][0:M_ROW, h0 + n, P * t:P * t + P],
                           ks[b % 2][0:M_ROW, h0 + n, 0:W], start=(n == 0), stop=False)
                    dst = ps_a[i][:, 0:nh * W].rearrange("p (n w) -> p n w", n=nh)[:, :, W - P:W]
                    mm(dst, identb[:, :], mask[:, 0:nh, :], start=False).then_inc(a_filled[i], 1)
                if kind == "negmax":
                    i = take(pe, ring_a, a_freed, s)
                    for n in (2, 1):
                        read(pe, ring_a, a_freed, ("max", b, G * NM - n))
                    for t in range(T):
                        last = turn(ps_a[i][0:H, P * t:P * t + P], mx[:, t, :])
                    last.then_inc(a_filled[i], 1)
                if kind == "score":
                    _, _, g, u = s
                    n = (b * G + g) * NS + u
                    if g == 0 and u == 0:
                        pe.wait_ge(nm_in[b % 2], 16 * PARTS * (b // 2 + 1))
                    if n >= 2:
                        pe.wait_ge(probs, n - 1)
                    for h, kt, c in score_parts(u):
                        hh = GH * g + h
                        last = mm(ps_b[n % 2][:, c:c + S - P * kt],
                                  ks[b % 2][0:M_ROW + PARTS, hh, P * kt:P * kt + P],
                                  qs[b % 2][0:M_ROW + PARTS, hh, P * kt:S])
                    last.then_inc(scores, 1)
                if kind == "pv":
                    _, _, g, c = s
                    kt = (0, 1, 3, 2)[c]
                    half, second = g // 2, g % 2
                    if c == 0:
                        read(pe, ring_a, a_freed, ("v", b))
                        if b == 0 and g == 0:
                            pe.wait_ge(biases, 2)
                        if not second and b:
                            pe.wait_ge(ctx_sb, 2 * (b - 1) + half + 1)
                            if half == 0:
                                pe.wait_ge(y_ready, b)
                    pe.wait_ge(masked, (b * G + g) * NS + (4, 8, 8, 10)[c])
                    for j in range(GH):
                        u, off = ((j, 0), (4 + j, 0), (8 + j // 2, 2 * P * (j % 2)), (4 + j, S - P))[kt]
                        w = S - P * kt
                        last = mm(ps_v[half][32 * j:32 * j + 32, P * kt:S], vp[b % 2][:, kt, GH * g + j, :],
                                  pr[:, prob_slot(b, g, u), off:off + w],
                                  start=(not second and c == 0), stop=bool(second and c == NPV - 1))
                    last.then_inc(pv_done, 1)
                if kind == "ctx_tok":
                    i = take(pe, ring_m, m_freed, s)
                    pe.wait_ge(ctx_sb, 2 * b + s[2] + 1)
                    for t in range(T):
                        last = turn(ps_m[i][:, P * t:P * t + P], cu[:, s[2], P * t:P * t + P])
                    last.then_inc(m_filled[i], 1)
                if kind == "ctxT":
                    i = take(pe, ring_m, m_freed, s)
                    for half in range(2):
                        read(pe, ring_m, m_freed, ("ctx_tok", b, half))
                    for t in range(T):
                        last = turn(ps_m[i][:, P * t:P * t + P], ctok[:, t, :])
                    last.then_inc(m_filled[i], 1)
                if kind == "out_proj":
                    i = take(pe, ring_m, m_freed, s)
                    read(pe, ring_m, m_freed, ("ctxT", b))
                    pe.wait_ge(ffn_in, 16 * FFN_LOADS)
                    for t in range(T):
                        last = mm(ps_m[i][:, P * t:P * t + P], dT[:, P * t:P * t + P], wo[:, :])
                    last.then_inc(m_filled[i], 1)
                if kind == "x1T":
                    i = take(pe, ring_m, m_freed, s)
                    pe.wait_ge(xn2_ready, T * (b + 1))
                    for t in range(T):
                        last = turn(ps_m[i][:, P * t:P * t + P], xn2[:, t, :])
                    last.then_inc(m_filled[i], 1)
                if kind == "enc":
                    c = s[2]
                    i = take(pe, ring_m, m_freed, s)
                    read(pe, ring_m, m_freed, ("x1T", b))
                    mm(ps_m[i][:, :], w_enc[:, P * c:P * c + P], dT[:, :]).then_inc(m_filled[i], 1)
                if kind == "s2c":
                    i = take(pe, ring_m, m_freed, s)
                    for c in range(HC):
                        read(pe, ring_m, m_freed, ("enc", b, c))
                        last = mm(ps_m[i][M * c:M * c + M, :], w_s2c[:, c, :], spikes[:, c, :])
                    last.then_inc(m_filled[i], 1)
                if kind == "router":
                    i = take(pe, ring_m, m_freed, s)
                    read(pe, ring_m, m_freed, ("s2c", b))
                    for t in range(T):
                        last = mm(ps_m[i][:, E * t:E * t + E], cont[:, P * t:P * t + P], wr[:, :])
                    last.then_inc(m_filled[i], 1)
                if kind == "w1":
                    i = take(pe, ring_m, m_freed, s)
                    mm(ps_m[i][:, :], w1[:, s[2], :], cont[:, :]).then_inc(m_filled[i], 1)
                if kind == "gateT":
                    i = take(pe, ring_m, m_freed, s)
                    pe.wait_ge(routed, ROUTE * (b + 1))
                    for t in range(T):
                        last = turn(ps_m[i][0:E, P * t:P * t + P], gate[:, t, :])
                    last.then_inc(m_filled[i], 1)
                if kind == "gate":
                    i = take(pe, ring_m, m_freed, s)
                    if s[2] == 0:
                        pe.wait_ge(gate_split, 5 * (b + 1))
                    mm(ps_m[i][:, :], sel[:, s[2], :], gs[:, :]).then_inc(m_filled[i], 1)
                if kind == "w2":
                    e = s[2]
                    if e == 0:
                        pe.wait_ge(ctx_sb, 2 * (b + 1))
                        pe.wait_ge(b2_split, 4)
                    read(pe, ring_m, m_freed, ("gate", b, e))
                    lo = M * (e % 2)
                    last = mm(ps_v[0][lo:lo + M, :], w2[:, e, :], hs[:, e, :], start=(e < 2), stop=(e == E - 1))
                    if e == E - 2:
                        for i in range(PARTS):
                            mm(ps_v[0][0:M, :], b2s[:, i, :], gs[:, :], start=False, stop=(i == PARTS - 1))
                    if e == E - 1:
                        last.then_inc(y_filled, 1)
                if kind == "c2s":
                    i = take(pe, ring_m, m_freed, s)
                    pe.wait_ge(y_ready, b + 1)
                    mm(ps_m[i][:, :], w_c2s[:, P * s[2]:P * s[2] + P], cont[:, :]).then_inc(m_filled[i], 1)
                if kind == "dec":
                    i = take(pe, ring_m, m_freed, s)
                    for c in range(HC):
                        read(pe, ring_m, m_freed, ("c2s", b, c))
                    for t in range(T):
                        for c in range(HC):
                            last = mm(ps_m[i][:, P * t:P * t + P], spikes[:, c, P * t:P * t + P], w_dec[:, c, :],
                                      start=(c == 0), stop=(c == HC - 1))
                    last.then_inc(m_filled[i], 1)

        @block.vector
        def _(dve):
            def stats(src, st, mv, done, b):
                for t in range(T):
                    nc.vector.bn_stats(st[:, t, :], src[:, t, :]).then_inc(done, 1)
                for t in range(T):
                    dve.wait_ge(done, 2 * T * b + T + t)
                    nc.vector.bn_aggr(mv[:, t, :], st[:, t, :]).then_inc(done, 1)

            def apply_norm(dst, src, mv, rs, done):
                for t in range(T):
                    nc.vector.tensor_scalar(dst[:, t, :], src[:, t, :], mv[:, t, 0:1], rs[:, t:t + 1],
                                            ALU.subtract, ALU.mult).then_inc(done, 1)

            def split3(f, p1, r, p2, p3, done, before):
                nc.vector.tensor_copy(p1, f).then_inc(done, 1)
                dve.wait_ge(done, before + 1)
                nc.vector.tensor_tensor(r, f, p1, ALU.subtract).then_inc(done, 1)
                dve.wait_ge(done, before + 2)
                nc.vector.tensor_copy(p2, r).then_inc(done, 1)
                dve.wait_ge(done, before + 3)
                nc.vector.tensor_tensor(p3, r, p2, ALU.subtract).then_inc(done, 1)

            nc.vector.memset(ones[:, :], 1.0).then_inc(ones_ready, 1)
            nc.vector.memset(gs[:, :], 0.0).then_inc(ones_ready, 1)

            def route(b):
                base = ROUTE * b
                done = [0]

                def wide(x):
                    return x[:, :].unsqueeze(2).to_broadcast([P, T, E])

                def then(ins):
                    ins.then_inc(routed, 1)
                    done[0] += 1
                    dve.wait_ge(routed, base + done[0])

                def tt(dst, x, w, op):
                    then(nc.vector.tensor_tensor(dst[:, :, :], x[:, :, :], w, op))

                def reduce(src, op):
                    then(nc.vector.tensor_reduce(r1[:, :], src[:, :, :], AX_X, op))

                reduce(lg, ALU.max)
                tt(lg, lg, wide(r1), ALU.subtract)
                dve.wait_ge(route_exp, b + 1)
                reduce(ex, ALU.max)
                tt(ra, ex, wide(r1), ALU.is_equal)
                tt(ra, ra, tie_rank[:, :, :], ALU.mult)
                reduce(ra, ALU.max)
                tt(oh1, ra, wide(r1), ALU.is_equal)
                then(nc.vector.scalar_tensor_tensor(out=rb[:, :, :], in0=oh1[:, :, :], scalar=-2.0, in1=ex[:, :, :],
                                                    op0=ALU.mult, op1=ALU.add))
                reduce(rb, ALU.max)
                tt(ra, rb, wide(r1), ALU.is_equal)
                tt(ra, ra, tie_rank[:, :, :], ALU.mult)
                reduce(ra, ALU.max)
                tt(oh2, ra, wide(r1), ALU.is_equal)
                tt(oh1, oh1, oh2[:, :, :], ALU.add)
                tt(ra, ex, oh1[:, :, :], ALU.mult)
                reduce(ra, ALU.add)
                then(nc.vector.reciprocal(r1[:, :], r1[:, :]))
                tt(gate, ra, wide(r1), ALU.mult)
                assert done[0] == ROUTE

            for s in steps:
                kind, b = s[0], (s[1] if len(s) > 1 else 0)
                if kind == "norm1":
                    dve.wait_ge(x_in[b], 16)
                    xb = x_all[:, T * b:T * b + T, :]
                    stats(xb, st1, mv1, ln1, b)
                    dve.wait_ge(rstd1, 2 * (b + 1))
                    if b:
                        j, r = bank(ring_a, ("xT", b - 1))
                        dve.wait_ge(a_filled[j], r + 1)
                    apply_norm(xn, xb, mv1, rs1, xn_ready)
                if kind == "norm1" and b == 0:
                    dve.wait_ge(bias_in, 16 * 2 * DK)
                    nc.vector.tensor_scalar(bqs[:, :], bq_raw[:, :], QSCALE, None, ALU.mult).then_inc(bqs_ready, 1)
                if kind in ("q", "k"):
                    w = int(kind == "k")
                    read(dve, ring_a, a_freed, s)
                    if b:
                        dve.wait_ge(stacked[(b - 1) % 2], 16 * STACKS * ((b - 1) // 2 + 1))
                    split3(qkf[:, w, :], parts[:, w, 0, :], qkr[:, :], parts[:, w, 1, :], parts[:, w, 2, :],
                           qk_split, 8 * b + 4 * w)
                if kind == "v":
                    i = full(dve, ring_a, a_filled, s)
                    if b == 0:
                        dve.wait_ge(vp_ones, 4)
                        dve.wait_ge(qkv_in, 16 * QKV_LOADS)
                    if b >= 2:
                        dve.wait_ge(pv_done, NPV * G * (b - 1))
                    for n in range(2):
                        heads = slice(GH * n, GH * n + GH)
                        src = ps_a[i][:, :].rearrange("p (a h k) -> p a h k", h=2 * GH, k=DK)[:, :, heads, :]
                        bias = bv[:, :, :].rearrange("p t (a h k) -> p (t a) h k", h=2 * GH, k=DK)[:, :, heads, :]
                        dst = vp[b % 2][:, :, :, :].rearrange("p t (a h) w -> p (t a) h w", h=2 * GH)
                        o = nc.vector.tensor_tensor(dst[:, :, heads, SLOT * n:SLOT * n + DK], src, bias, ALU.add)
                    o.then_inc(a_freed[i], 1)
                if kind == "ffn_setup":
                    dve.wait_ge(ffn_in, 16 * FFN_LOADS)
                    nc.vector.tensor_scalar(w_s2c[:, :, :], w_s2c[:, :, :], 0.5, None, ALU.mult).then_inc(halved, 1)
                    nc.vector.tensor_scalar(w_dec[:, :, :], w_dec[:, :, :], 0.5, None, ALU.mult).then_inc(halved, 1)
                    nc.vector.tensor_scalar(b_enc[:, :], b_enc[:, :], 0.5, None, ALU.mult).then_inc(halved, 1)
                    nc.vector.tensor_scalar(b_c2s[:, :], b_c2s[:, :], 0.5, None, ALU.mult).then_inc(halved, 1)
                    split3(b2f[:, :], b2s[:, 0, :], b2r[:, :], b2s[:, 1, :], b2s[:, 2, :], b2_split, 0)
                    dve.wait_ge(sums_ps, 1)
                    nc.vector.tensor_tensor(b_s2c[0:M, :], b_s2c[0:M, :], ps_m[0][0:M, 0:1], ALU.add
                                            ).then_inc(biases, 1)
                    nc.vector.tensor_tensor(b_dec[:, :], b_dec[:, :], ps_v[0][:, 0:D], ALU.add).then_inc(biases, 1)
                if kind == "max":
                    t, h0, nh = MU[s[2]]
                    i = full(dve, ring_a, a_filled, s)
                    W = P * (t + 1)
                    src = ps_a[i][:, 0:nh * W].rearrange("p (n w) -> p n w", n=nh)
                    nc.vector.tensor_reduce(mx[:, t, h0:h0 + nh], src, AX_X, ALU.max).then_inc(a_freed[i], 1)
                if kind == "negmax":
                    i = full(dve, ring_a, a_filled, s)
                    nc.vector.tensor_scalar(nmf[:, :], ps_a[i][0:H, :], -1.0, None, ALU.mult).then_inc(a_freed[i], 1)
                    read(dve, ring_a, a_freed, s)
                    if b:
                        dve.wait_ge(nm_in[(b - 1) % 2], 16 * PARTS * ((b - 1) // 2 + 1))
                    split3(nmf[:, :], nmp[:, 0, :], nmr[:, :], nmp[:, 1, :], nmp[:, 2, :], nm_split, 4 * b)
                if kind == "ctx_tok":
                    half = s[2]
                    i = full(dve, ring_m, m_filled, s)
                    v = ps_m[i][:, :].rearrange("p (t j c) -> p t j c", t=T, c=VW)
                    if b or half:
                        read(dve, ring_m, m_freed, ("ctx_tok", b - 1, 1) if half == 0 else ("ctx_tok", b, 0))
                    nc.vector.reciprocal(rsum[:, :, :, :], v[:, :, :, DK:DK + SLOT + 1:SLOT]).then_inc(recip, 1)
                    dve.wait_ge(recip, 2 * b + half + 1)
                    if half == 0 and b:
                        j, r = bank(ring_m, ("ctxT", b - 1))
                        dve.wait_ge(m_filled[j], r + 1)
                    dst = ctok[:, :, :].rearrange("p t (a j k) -> p a t j k", j=GH, k=DK)
                    for n in range(2):
                        o = nc.vector.tensor_tensor(
                            dst[:, 2 * half + n], v[:, :, :, SLOT * n:SLOT * n + DK],
                            rsum[:, :, :, n:n + 1].to_broadcast([P, T, GH, DK]), ALU.mult)
                    o.then_inc(m_freed[i], 1)
                if kind == "out_proj":
                    i = full(dve, ring_m, m_filled, s)
                    dve.wait_ge(x_bo, b + 1)
                    if b:
                        dve.wait_ge(x1_lnb, b)
                    nc.vector.tensor_tensor(x1[:, :, :], ps_m[i][:, :].rearrange("p (t d) -> p t d", t=T),
                                            x_all[:, T * b:T * b + T, :], ALU.add).then_inc(m_freed[i], 1)
                if kind == "norm2":
                    read(dve, ring_m, m_freed, ("out_proj", b))
                    stats(x1, st2, mv2, ln2, b)
                    dve.wait_ge(rstd2, 2 * (b + 1))
                    apply_norm(xn2, x1, mv2, rs2, xn2_ready)
                if kind == "router":
                    i = full(dve, ring_m, m_filled, s)
                    nc.vector.tensor_tensor(lg[:, :, :], ps_m[i][:, 0:T * E].rearrange("p (t e) -> p t e", t=T),
                                            br[:, :, :], ALU.add).then_inc(m_freed[i], 1)
                    read(dve, ring_m, m_freed, s)
                    route(b)
                if kind == "gateT":
                    i = full(dve, ring_m, m_filled, s)
                    nc.vector.tensor_copy(nmf[0:E, :], ps_m[i][0:E, :]).then_inc(m_freed[i], 1)
                    read(dve, ring_m, m_freed, s)
                    if b:
                        dve.wait_ge(y_filled, b)
                    split3(nmf[0:E, :], gs[0:E, :], nmr[0:E, :], g2[:, :], gs[64:64 + E, :], gate_split, 5 * b)
                    nc.vector.tensor_copy(gs[32:32 + E, :], g2[:, :]).then_inc(gate_split, 1)
                if kind == "gate":
                    e = s[2]
                    i = full(dve, ring_m, m_filled, s)
                    read(dve, ring_m, m_freed, ("w1", b, e))
                    nc.vector.tensor_tensor(hs[:, e, :], ps_m[i][:, :], hs[:, e, :], ALU.mult
                                            ).then_inc(m_freed[i], 1)
                if kind == "dec":
                    i = full(dve, ring_m, m_filled, s)
                    if b:
                        dve.wait_ge(stored, 16 * b)
                    nc.vector.tensor_tensor(z[:, :, :], ps_m[i][:, :].rearrange("p (t d) -> p t d", t=T),
                                            b_dec[:, :].unsqueeze(1).to_broadcast([P, T, D]), ALU.add
                                            ).then_inc(m_freed[i], 1)
                    read(dve, ring_m, m_freed, s)
                    stats(z, st3, mv3, ln3, b)
                    dve.wait_ge(rstd3, 2 * (b + 1))
                    apply_norm(xn2, z, mv3, rs3, zn_ready)
                    dve.wait_ge(zn_scaled, b + 1)
                    dve.wait_ge(x1_lnb, b + 1)
                    nc.vector.tensor_tensor(z[:, :, :], xn2[:, :, :], x_all[:, T * b:T * b + T, :], ALU.add).then_inc(res_ready, 1)


_INS = ["L0_attn_embeddings", "L0_attn_Wq", "L0_attn_bq", "L0_attn_Wk", "L0_attn_bk", "L0_attn_Wv", "L0_attn_bv",
        "L0_attn_Wo", "L0_attn_bo", "L0_ffn_W_enc", "L0_ffn_b_enc", "L0_ffn_W_s2c", "L0_ffn_b_s2c", "L0_ffn_Wr",
        "L0_ffn_br", "L0_ffn_W1", "L0_ffn_b1", "L0_ffn_W2", "L0_ffn_b2", "L0_ffn_W_c2s", "L0_ffn_b_c2s",
        "L0_ffn_W_dec", "L0_ffn_b_dec", "L0_ffn_ln_g", "L0_ffn_ln_b"]


def kernel(**inputs):
    import numpy as np
    from concourse import bacc
    from concourse.bass_utils import run_bass_kernel_spmd

    nc = bacc.Bacc("TRN2", target_bir_lowering=False, num_devices=1)
    arrays, aps = {}, {}
    for name in _INS:
        arrays[f"in_{name}"] = np.ascontiguousarray(inputs[name])
        aps[name] = nc.dram_tensor(f"in_{name}", arrays[f"in_{name}"].shape, F32, kind="ExternalInput").ap()
    out = nc.dram_tensor("out", arrays["in_L0_attn_embeddings"].shape, F32, kind="ExternalOutput").ap()
    build(nc, aps, out)
    return run_bass_kernel_spmd(nc, [arrays], core_ids=[0]).results[0]["out"]
```

```python
from contextlib import ExitStack

import concourse.bass as bass
from concourse import mybir

ALU = mybir.AluOpType
ACT = mybir.ActivationFunctionType
F32 = mybir.dt.float32
BF16 = mybir.dt.bfloat16
AX_X = mybir.AxisListType.X

P = 128
EPS = 1e-5
MASKED = -1e30
PARTS = 3
M_ROW = 96
M_PARTS = 2


def max_units(tiles, group):
    units = []
    for t in reversed(range(tiles)):
        n = max(1, tiles // (t + 1)) if (t + 1) * group > tiles else group
        n = min(n, group)
        units += [(t, h, n) for h in range(0, group, n)]
    return units


def attention_steps(b, groups, n_score):
    steps = []
    for g in range(groups + 1):
        for u in range(n_score):
            if g < groups:
                steps.append(("score", b, g, u))
            if g and u in (2, 5, 7, 9):
                steps.append(("pv", b, g - 1, (2, 5, 7, 9).index(u)))
            if g == 2 and u == 9:
                steps.append(("ctx_out", b, 0))
            if g == 3 and u == 2:
                steps.append(("ctx_tok", b, 0))
    return steps + [("ctx_out", b, 1), ("ctx_tok", b, 1), ("ctxT", b), ("out_proj", b), ("stats2", b), ("norm2", b)]


def expert_steps(b):
    w1 = [("w1", b, e) for e in range(8)]
    pair = [[("gate", b, p), ("w2", b, p)] for p in range(4)]
    return ([("x1T", b), ("enc", b, 0), ("enc", b, 1), ("s2c", b), ("router", b)] + w1[0:6] + [("gateT", b)] + pair[0]
            + pair[1] + w1[6:7] + pair[2] + w1[7:8] + pair[3]
            + [("c2s", b, 0), ("c2s", b, 1), ("dec", b), ("norm3", b), ("result", b)])


def front_steps(b):
    return [(what, b) for what in ("stats1", "norm1", "xT", "q", "k", "v")]


def merge(*streams):
    placed = []
    for order, (steps, lo, hi) in enumerate(streams):
        placed += [(lo + (hi - lo) * (i + 0.5) / len(steps), order, i, s) for i, s in enumerate(steps)]
    return [s for *_, s in sorted(placed)]


def schedule(B, groups, n_max, n_score):
    def maxima(b, g0, g1):
        return [("max", b, n) for n in range(g0 * n_max, g1 * n_max)]

    first = front_steps(0) + maxima(0, 0, 1) + [("negmax", 0, 0, 1)]
    yield from first
    ahead = maxima(0, 1, 2) + [("negmax", 0, 1, 2)] + maxima(0, 2, groups) + [("negmax", 0, 2, groups), ("ffn_setup",)]
    attend = attention_steps(0, groups, n_score)
    cut = [attend.index(("score", 0, g, 0)) for g in (1, 2)]
    yield from ahead[0:n_max + 1]
    yield from merge((attend[0:cut[1]], 0.0, 1.0), (ahead[n_max + 1:], 0.0, 1.0), (front_steps(1), 0.3, 1.0))
    rest = attend[cut[1]:]
    yield from merge((rest, 0.0, 1.0), (maxima(1, 0, groups), 0.1, 0.9))
    yield ("negmax", 1, 0, groups)
    for b in range(1, B):
        streams = [(attention_steps(b, groups, n_score), 0.0, 1.0), (expert_steps(b - 1), 0.0, 0.95)]
        if b + 1 < B:
            streams += [(front_steps(b + 1), 0.0, 0.15), (maxima(b + 1, 0, groups), 0.3, 0.93),
                        ([("negmax", b + 1, 0, groups)], 0.95, 0.95)]
        yield from merge(*streams)
    yield from expert_steps(B - 1)


def build(nc, a, out):
    B, S, D = a["L0_attn_embeddings"].shape
    H, _, DK = a["L0_attn_Wq"].shape
    HID = a["L0_ffn_W_enc"].shape[1]
    M = a["L0_ffn_W_s2c"].shape[1]
    E, _, EH = a["L0_ffn_W1"].shape
    T = S // P
    HC = HID // P
    GH = 4
    G = H // GH
    NS = 10
    SLOTS = 14
    HS = 6
    NPV = 4
    QSCALE = float(DK) ** -0.5
    VW = 32
    SLOT = DK + 1
    assert (D, EH, S, H * DK, 2 * M, GH) == (P, P, 512, P, P, T)

    MU = []
    for g in range(G):
        MU += [(t, GH * g + h, n) for t, h, n in max_units(T, GH)]
    NM = len(MU) // G
    steps = list(schedule(B, G, NM, NS))

    ring_a = {s: n for n, s in enumerate([s for s in steps if s[0] in ("xT", "q", "k", "v", "max", "negmax")])}
    ring_m = {s: n for n, s in enumerate([s for s in steps if s[0] in (
        "ffn_setup",         "ctx_tok", "ctxT", "out_proj", "x1T", "enc", "s2c", "router", "w1", "gateT", "gate", "w2", "c2s", "dec")])}
    order_negmax = {s: n for n, s in enumerate([s for s in steps if s[0] == "negmax"])}
    assert E == 8 and G == T

    with ExitStack() as ctx:
        def sb(name, shape, dt=F32):
            return ctx.enter_context(nc.sbuf_tensor(name, shape, dt))

        def sem(name):
            return ctx.enter_context(nc.semaphore(name))

        ps_a = [ctx.enter_context(nc.psum_tensor(f"ps_a{i}", [P, 512], F32)) for i in range(2)]
        ps_b = [ctx.enter_context(nc.psum_tensor(f"ps_b{i}", [P, 512], F32)) for i in range(2)]
        ps_v = [ctx.enter_context(nc.psum_tensor(f"ps_v{i}", [P, 512], F32)) for i in range(2)]
        ps_m = [ctx.enter_context(nc.psum_tensor(f"ps_m{i}", [P, 512], F32)) for i in range(2)]

        ident = sb("ident", [P, P])
        identb = sb("identb", [P, P], BF16)
        mask = sb("mask", [P, 4, P], BF16)
        ones = sb("ones", [P, P])
        minus_half = sb("minus_half", [P, T])
        tie_rank = sb("tie_rank", [P, T, E])
        sel = sb("sel", [M_ROW, E // 2, 2, M], BF16)
        x_all = sb("x_all", [P, B * T, D])
        w_qk_raw = sb("w_qk_raw", [P, 2, H, DK])
        w_qk = sb("w_qk", [P, 2, DK, H])
        wv = sb("wv", [P, H, DK])
        bq_raw = sb("bq_raw", [P, 1])
        bqs = sb("bqs", [P, 1])
        bk = sb("bk", [P, 1])
        bv = sb("bv", [P, T, H * DK])
        wo = sb("wo", [P, D])
        bo = sb("bo", [P, D])
        w_enc = sb("w_enc", [P, HID])
        b_enc = sb("b_enc", [P, HC])
        w_s2c = sb("w_s2c", [P, HC, M])
        b_s2c = sb("b_s2c", [P, 1])
        wr = sb("wr", [P, E])
        br = sb("br", [P, T, E])
        zeros_b = sb("zeros_b", [M_ROW - PARTS * PARTS * DK, S], BF16)
        minus_b = sb("minus_b", [M_PARTS, S], BF16)
        w1 = sb("w1", [P, E, EH])
        b1 = sb("b1", [P, E])
        w2 = sb("w2", [P, E, M])
        b2 = sb("b2", [P, E // 2])
        w_c2s = sb("w_c2s", [P, HID])
        b_c2s = sb("b_c2s", [P, HC])
        w_dec = sb("w_dec", [P, HC, D])
        b_dec = sb("b_dec", [P, D])
        ln_g = sb("ln_g", [P, D])
        ln_b = sb("ln_b", [P, D])

        st1 = sb("st1", [P, T, 6])
        mv1 = sb("mv1", [P, T, 2])
        rs1 = sb("rs1", [P, T])
        xn = sb("xn", [P, T, D])
        xT = sb("xT", [P, S])
        qkf = sb("qkf", [P, 2, S])
        qkr = sb("qkr", [P, S])
        parts = sb("parts", [P, 2, PARTS, S], BF16)
        qs = [sb(f"qs{i}", [P, H, S], BF16) for i in range(2)]
        ks = [sb(f"ks{i}", [P, H, S], BF16) for i in range(2)]
        vp = [sb(f"vp{i}", [P, T, H, VW]) for i in range(2)]
        mx = sb("mx", [P, T, H])
        nmf = sb("nmf", [H, S])
        nmp = sb("nmp", [H, M_PARTS, S], BF16)
        pr = sb("pr", [P, SLOTS, S])
        cu = sb("cu", [P, 2, S])
        rsum = sb("rsum", [P, T, GH, 2])
        ctok = sb("ctok", [P, T, H * DK])
        dT = sb("dT", [P, S])

        x1 = sb("x1", [P, T, D])
        st2 = sb("st2", [P, T, 6])
        mv2 = sb("mv2", [P, T, 2])
        rs2 = sb("rs2", [P, T])
        xn2 = sb("xn2", [P, T, D])
        spikes = sb("spikes", [P, HC, S])
        cont = sb("cont", [P, S])
        lg = sb("lg", [P, T, E])
        ex = sb("ex", [P, T, E])
        ra = sb("ra", [P, T, E])
        rb = sb("rb", [P, T, E])
        oh1 = sb("oh1", [P, T, E])
        oh2 = sb("oh2", [P, T, E])
        r1 = sb("r1", [P, T])
        gate = sb("gate", [P, T, E])
        gf = sb("gf", [E, S])
        gr = sb("gr", [E, S])
        g2 = sb("g2", [E, S], BF16)
        gs = sb("gs", [M_ROW, S], BF16)
        hs = sb("hs", [P, HS, S])
        gb = sb("gb", [P, E // 2, S])
        z = sb("z", [P, T, D])
        st3 = sb("st3", [P, T, 6])
        mv3 = sb("mv3", [P, T, 2])
        rs3 = sb("rs3", [P, T])

        x_in = [sem(f"x_in{b}") for b in range(B)]
        w_qk_in = sem("w_qk_in")
        qkv_in = sem("qkv_in")
        ffn_in = sem("ffn_in")
        filled = sem("filled")
        consts = sem("consts")
        vp_ones = sem("vp_ones")
        rows_set = [sem(f"rows_set{i}") for i in range(2)]
        ones_ready = sem("ones_ready")
        bias_in = sem("bias_in")
        bqs_ready = sem("bqs_ready")
        w_turned = sem("w_turned")
        halved = sem("halved")
        sums_ps = sem("sums_ps")
        biases = sem("biases")
        a_filled = [sem(f"a_filled{i}") for i in range(2)]
        a_freed = [sem(f"a_freed{i}") for i in range(2)]
        m_filled = [sem(f"m_filled{i}") for i in range(2)]
        m_freed = [sem(f"m_freed{i}") for i in range(2)]
        ln1 = sem("ln1")
        rstd1 = sem("rstd1")
        xn_ready = sem("xn_ready")
        x_bo = sem("x_bo")
        qk_high = sem("qk_high")
        qk_split = sem("qk_split")
        gate_high = sem("gate_high")
        in_dram = [[sem(f"in_dram{b}{w}") for w in "qk"] for b in range(B)]
        stacked = [sem(f"stacked{i}") for i in range(B + 1)]
        nm_split = sem("nm_split")
        nm_in = [sem(f"nm_in{i}") for i in range(len(order_negmax))]
        scores = sem("scores")
        probs = sem("probs")
        masked = sem("masked")
        pv_done = sem("pv_done")
        ctx_sb = sem("ctx_sb")
        recip = sem("recip")
        ln2 = sem("ln2")
        rstd2 = sem("rstd2")
        xn2_ready = sem("xn2_ready")
        x1_lnb = sem("x1_lnb")
        routed = sem("routed")
        route_exp = sem("route_exp")
        gate_split = sem("gate_split")
        w2_pool = sem("w2_pool")
        w2_sum = sem("w2_sum")
        y_ready = sem("y_ready")
        ln3 = sem("ln3")
        rstd3 = sem("rstd3")
        zn_ready = sem("zn_ready")
        zn_scaled = sem("zn_scaled")
        res_ready = sem("res_ready")
        stored = sem("stored")

        SPLIT = 6
        ROUTE = 18

        parts_dram = nc.dram_tensor("parts_dram", [B, 2, PARTS, P * S], BF16, kind="Internal").ap()
        pieces = [[(0, 0, GH), (1, GH, H)]] + [[(b + 1, 0, H)] for b in range(1, B)]
        STACK_DMAS = 1 + PARTS

        def bank(ring, s):
            n = ring[s]
            return n % 2, n // 2

        def take(eng, ring, freed, s):
            i, r = bank(ring, s)
            if r:
                eng.wait_ge(freed[i], r)
            return i

        def read(eng, ring, freed, s):
            i, r = bank(ring, s)
            eng.wait_ge(freed[i], r + 1)

        def full(eng, ring, filled, s):
            i, r = bank(ring, s)
            eng.wait_ge(filled[i], r + 1)
            return i

        def score_parts(u):
            if u < 4:
                return [(u, 0, 0)]
            if u < 8:
                return [(u - 4, 1, 0), (u - 4, 3, S - P)]
            return [(2 * (u - 8) + i, 2, i * 2 * P) for i in range(2)]

        def prob_slot(b, g, u):
            return ((b * G + g) * NS + u) % SLOTS

        def pv_count(n):
            return NPV * (n // NS) + (1, 3, 4)[n % NS // 4]

        block = ctx.enter_context(nc.Block())

        def rows(x):
            return x.partition_broadcast(P)

        ffn_loads = [
            (w_s2c[:, :, :], a["L0_ffn_W_s2c"].rearrange("(c p) m -> p c m", p=P)),
            (b_s2c[0:M, :], a["L0_ffn_b_s2c"].unsqueeze(1)),
            (w_dec[:, :, :], a["L0_ffn_W_dec"].rearrange("(c p) d -> p c d", p=P)),
            (b_dec[:, :], rows(a["L0_ffn_b_dec"])),
            (b_enc[:, :], a["L0_ffn_b_enc"].rearrange("(c p) -> p c", p=P)),
            (b_c2s[:, :], a["L0_ffn_b_c2s"].rearrange("(c p) -> p c", p=P)),
            (wo[:, :], a["L0_attn_Wo"]),
            (w_enc[:, :], a["L0_ffn_W_enc"]),
            (b1[:, :], a["L0_ffn_b1"].rearrange("e h -> h e")),
            (w2[:, :, :], a["L0_ffn_W2"].rearrange("e h m -> h e m")),
            (ln_g[:, :], rows(a["L0_ffn_ln_g"])),
            (ln_b[:, :], rows(a["L0_ffn_ln_b"])),
        ]
        for t in range(T):
            ffn_loads.append((br[:, t, :], rows(a["L0_ffn_br"])))
        for i in range(2):
            half = slice(M * i, M * i + M)
            ffn_loads += [
                (wr[half, :], a["L0_ffn_Wr"]),
                (w1[half, :, :], a["L0_ffn_W1"].rearrange("e m h -> m e h")),
                (w_c2s[half, :], a["L0_ffn_W_c2s"]),
                (b2[half, :], a["L0_ffn_b2"].rearrange("(p i) m -> i m p", i=2)[i]),
            ]

        @block.sync
        def _(sp):
            x_dram = a["L0_attn_embeddings"].rearrange("b (t p) d -> p b t d", p=P)
            with nc.allow_non_contiguous_dma(reason="small transposed biases"):
                sp.dma_start(x_all[:, 0:T, :], x_dram[:, 0]).then_inc(x_in[0], 16)
                sp.dma_start(w_qk_raw[:, 1], a["L0_attn_Wk"].rearrange("h d k -> d h k")).then_inc(w_qk_in, 16)
                sp.dma_start(wv[:, :, :], a["L0_attn_Wv"].rearrange("h d k -> d h k")).then_inc(qkv_in, 16)
                for t in range(T):
                    sp.dma_start(bv[:, t, :], rows(a["L0_attn_bv"].rearrange("h k -> (h k)"))).then_inc(qkv_in, 16)
                sp.dma_start(bo[:, :], rows(a["L0_attn_bo"])).then_inc(qkv_in, 16)
            sp.wait_ge(filled, 3)
            r0 = PARTS * PARTS * DK

            def constant_rows(i):
                for st in (qs[i], ks[i]):
                    sp.dma_start(st[r0:M_ROW, :, :], zeros_b[:, :].unsqueeze(1).to_broadcast([M_ROW - r0, H, S])
                                 ).then_inc(rows_set[i], 16)
                sp.dma_start(ks[i][M_ROW:M_ROW + M_PARTS, :, :],
                             minus_b[:, :].unsqueeze(1).to_broadcast([M_PARTS, H, S])).then_inc(rows_set[i], 16)

            constant_rows(0)
            for s in steps:
                if s[0] in ("q", "k"):
                    b, w = s[1], int(s[0] == "k")
                    sp.wait_ge(qk_split, SPLIT * b + 3 * (w + 1))
                    sp.dma_start(parts_dram[b, w].rearrange("i (p t) -> p i t", p=P), parts[:, w, :, :]
                                 ).then_inc(in_dram[b][w], 16)
                if s[0] == "k":
                    for w in range(2):
                        sp.wait_ge(in_dram[b][w], 16)
                    if b >= 2:
                        sp.wait_ge(pv_done, NPV * G * (b - 1))
                    for n, h0, h1 in pieces[b]:
                        src = parts_dram[b, 0].rearrange("i (d h t) -> (i d) h t", d=DK, h=H)[:, h0:h1, :]
                        sp.dma_start(qs[b % 2][0:r0, h0:h1, :],
                                     src.unsqueeze(0).to_broadcast([PARTS, PARTS * DK, h1 - h0, S])
                                     ).then_inc(stacked[n], 16)
                        for i in range(PARTS):
                            src = parts_dram[b, 1, i].rearrange("(d h t) -> d h t", d=DK, h=H)[:, h0:h1, :]
                            sp.dma_start(ks[b % 2][PARTS * DK * i:PARTS * DK * (i + 1), h0:h1, :],
                                         src.unsqueeze(0).to_broadcast([PARTS, DK, h1 - h0, S])
                                         ).then_inc(stacked[n], 16)
                    if b == 0:
                        for n in range(1, B):
                            sp.dma_start(x_all[:, T * n:T * n + T, :], x_dram[:, n]).then_inc(x_in[n], 16)
                        constant_rows(1)
                if s[0] == "negmax":
                    _, b, g0, g1 = s
                    n = order_negmax[s]
                    read(sp, ring_a, a_freed, s)
                    for part in range(M_PARTS):
                        sp.dma_start(qs[b % 2][M_ROW + part:M_ROW + part + 1, GH * g0:GH * g1, :],
                                     nmp[0:GH * (g1 - g0), part, :]).then_inc(nm_in[n], 16)
                if s[0] == "result":
                    b = s[1]
                    sp.wait_ge(res_ready, b + 1)
                    sp.dma_start(out.rearrange("b (t p) d -> p b t d", p=P)[:, b], z[:, :, :]).then_inc(stored, 16)
            sp.wait_ge(stored, 16 * B)

        @block.gpsimd
        def _(pool):
            nc.gpsimd.memset(minus_half[:, :], -0.5).then_inc(filled, 1)
            nc.gpsimd.memset(zeros_b[:, :], 0.0).then_inc(filled, 1)
            nc.gpsimd.memset(minus_b[:, :], -1.0).then_inc(filled, 1)
            nc.gpsimd.memset(b_s2c[:, :], 0.0).then_inc(filled, 1)
            for t_ in (ident, identb, mask):
                nc.gpsimd.memset(t_[:], 0.0).then_inc(filled, 1)
            pool.wait_ge(filled, 7)
            nc.gpsimd.affine_select(out=ident[:, :], in_=ident[:, :], compare_op=ALU.not_equal, fill=1.0, base=0,
                                    pattern=[[-1, P]], channel_multiplier=1).then_inc(consts, 1)

            def masks():
                nc.gpsimd.affine_select(out=identb[:, :], in_=identb[:, :], compare_op=ALU.not_equal, fill=1.0,
                                        base=0, pattern=[[-1, P]], channel_multiplier=1).then_inc(consts, 1)
                nc.gpsimd.affine_select(out=mask[:, :, :], in_=mask[:, :, :], compare_op=ALU.is_ge, fill=MASKED,
                                        base=0, pattern=[[0, 4], [-1, P]], channel_multiplier=1).then_inc(consts, 1)

            def padded_values():
                for n in range(2):
                    nc.gpsimd.memset(vp[n][:, :, :, :], 0.0).then_inc(filled, 1)
                pool.wait_ge(filled, 9)
                for n in range(2):
                    for second in range(2):
                        v = vp[n][:, :, :, :].rearrange("p t (a h) w -> p (t a) h w", h=2 * GH)
                        c = SLOT * second + DK
                        nc.gpsimd.memset(v[:, :, GH * second:GH * second + GH, c:c + 1], 1.0).then_inc(vp_ones, 1)

            def selectors():
                nc.gpsimd.memset(sel[:, :, :, :], 0.0).then_inc(filled, 1)
                pool.wait_ge(filled, 10)
                for i in range(PARTS):
                    v = sel[32 * i:32 * i + 32, :, :, :].rearrange("r p i m -> r (p i) m")
                    nc.gpsimd.affine_select(out=v, in_=v, compare_op=ALU.not_equal, fill=1.0, base=0,
                                            pattern=[[-1, E], [0, M]], channel_multiplier=1).then_inc(consts, 1)
                    pool.wait_ge(consts, 4 + i)
                for e in range(E):
                    nc.gpsimd.memset(tie_rank[:, :, e:e + 1], float(E - e)).then_inc(consts, 1)

            for s in steps:
                kind, b = s[0], (s[1] if len(s) > 1 else 0)
                if kind in ("stats1", "stats2", "dec"):
                    stats, rstd, mv, rs = {"stats1": (ln1, rstd1, mv1, rs1), "stats2": (ln2, rstd2, mv2, rs2),
                                           "dec": (ln3, rstd3, mv3, rs3)}[kind]
                    pool.wait_ge(stats, 2 * T * (b + 1))
                    nc.gpsimd.tensor_scalar(rs[:, :], mv[:, :, 1], EPS, None, ALU.add).then_inc(rstd, 1)
                    pool.wait_ge(rstd, 2 * b + 1)
                    nc.gpsimd.tensor_tensor(rs[:, :], rs[:, :], minus_half[:, :], ALU.pow).then_inc(rstd, 1)
                if kind == "stats1" and b == 0:
                    masks()
                    padded_values()
                if kind == "negmax" and order_negmax[s] == 0:
                    selectors()
                if kind == "v":
                    pool.wait_ge(xn_ready, T * (b + 1))
                    pool.wait_ge(qkv_in, 16 * (T + 2))
                    xb = x_all[:, T * b:T * b + T, :]
                    nc.gpsimd.tensor_tensor(xb, xb, bo[:, :].unsqueeze(1).to_broadcast([P, T, D]),
                                            ALU.add).then_inc(x_bo, 1)
                if kind == "score":
                    _, _, g, u = s
                    slot = pr[:, prob_slot(b, g, u), :]
                    pool.wait_ge(probs, (b * G + g) * NS + u + 1)
                    if u < 4:
                        n, v = 1, slot[:, 0:P].rearrange("p (a c) -> p a c", a=1)
                    elif u < 8:
                        n, v = 2, slot.rearrange("p (a c) -> p a c", c=P)[:, 0:4:3, :]
                    else:
                        n, v = 2, slot.rearrange("p (a c) -> p a c", a=2)[:, :, 0:P]
                    nc.gpsimd.affine_select(out=v, in_=v, compare_op=ALU.is_ge, fill=0.0, base=0,
                                            pattern=[[0, n], [1, P]], channel_multiplier=-1).then_inc(masked, 1)
                if kind == "stats2":
                    pool.wait_ge(ffn_in, 16 * len(ffn_loads))
                    read(pool, ring_m, m_freed, ("out_proj", b))
                    nc.gpsimd.tensor_tensor(x_all[:, T * b:T * b + T, :], x1[:, :, :], ln_b[:, :].unsqueeze(1).to_broadcast([P, T, D]),
                                            ALU.add).then_inc(x1_lnb, 1)
                if kind == "w2" and s[2] == 1:
                    for p_ in range(2):
                        read(pool, ring_m, m_freed, ("w2", b, p_))
                    nc.gpsimd.tensor_tensor(gb[:, 0, :], gb[:, 0, :], gb[:, 1, :], ALU.add).then_inc(w2_pool, 1)
                if kind == "norm3":
                    pool.wait_ge(zn_ready, T * (b + 1))
                    nc.gpsimd.tensor_tensor(xn2[:, :, :], xn2[:, :, :], ln_g[:, :].unsqueeze(1).to_broadcast([P, T, D]),
                                            ALU.mult).then_inc(zn_scaled, 1)

        @block.scalar
        def _(act):
            with nc.allow_non_contiguous_dma(reason="small transposed biases"):
                act.dma_start(w_qk_raw[:, 0], a["L0_attn_Wq"].rearrange("h d k -> d h k")).then_inc(w_qk_in, 16)
                for dst, name in ((bq_raw, "bq"), (bk, "bk")):
                    for k in range(DK):
                        act.dma_start(dst[H * k:H * k + H, :], a[f"L0_attn_{name}"][:, k:k + 1]).then_inc(bias_in, 16)
            act.wait_ge(w_qk_in, 32)
            nc.scalar.copy(w_qk[:, :, :, :], w_qk_raw[:, :, :, :].rearrange("p w h k -> p w k h")).then_inc(w_turned, 1)

            for s in steps:
                kind, b = s[0], (s[1] if len(s) > 1 else 0)
                if kind == "xT":
                    i = full(act, ring_a, a_filled, s)
                    if b:
                        j, r = bank(ring_a, ("v", b - 1))
                        act.wait_ge(a_filled[j], r + 1)
                    nc.scalar.copy(xT[:, :], ps_a[i][:, :]).then_inc(a_freed[i], 1)
                if kind in ("q", "k"):
                    w = int(kind == "k")
                    i = full(act, ring_a, a_filled, s)
                    act.wait_ge(bqs_ready, 1)
                    if b:
                        act.wait_ge(in_dram[b - 1][w], 16)
                    for dst, done in ((parts[:, w, 0, :], qk_high), (qkf[:, w, :], a_freed[i])):
                        nc.scalar.activation(dst, ps_a[i][:, :], ACT.Identity, bias=(bk if w else bqs)[:, 0:1],
                                             scale=1.0 if w else QSCALE).then_inc(done, 1)
                if kind == "v" and b == 0:
                    act.wait_ge(filled, 7)
                    with nc.allow_non_contiguous_dma(reason="small transposed biases"):
                        for dst, src in ffn_loads:
                            act.dma_start(dst, src).then_inc(ffn_in, 16)
                if kind == "score":
                    _, _, g, u = s
                    n = (b * G + g) * NS + u
                    act.wait_ge(scores, n + 1)
                    if n >= SLOTS:
                        act.wait_ge(pv_done, pv_count(n - SLOTS))
                    nc.scalar.activation(pr[:, prob_slot(b, g, u), :], ps_b[n % 2][:, :],
                                         ACT.Exp).then_inc(probs, 1)
                if kind == "ctx_out":
                    half = s[2]
                    act.wait_ge(pv_done, NPV * (b * G + 2 * (half + 1)))
                    if b:
                        j, r = bank(ring_m, ("ctx_tok", b - 1, half))
                        act.wait_ge(m_filled[j], r + 1)
                    nc.scalar.copy(cu[:, half, :], ps_v[half][:, :]).then_inc(ctx_sb, 1)
                if kind in ("ctxT", "x1T"):
                    i = full(act, ring_m, m_filled, s)
                    nc.scalar.copy(dT[:, :], ps_m[i][:, :]).then_inc(m_freed[i], 1)
                if kind in ("enc", "c2s"):
                    c = s[2]
                    if b == 0 and c == 0:
                        read(act, ring_m, m_freed, ("ffn_setup",))
                    i = full(act, ring_m, m_filled, s)
                    bias = b_enc if kind == "enc" else b_c2s
                    nc.scalar.activation(spikes[:, c, :], ps_m[i][:, :], ACT.Tanh, bias=bias[:, c:c + 1],
                                         scale=0.5).then_inc(m_freed[i], 1)
                if kind == "s2c":
                    i = full(act, ring_m, m_filled, s)
                    nc.scalar.activation(cont[:, :], ps_m[i][:, :], ACT.Identity,
                                         bias=b_s2c[:, 0:1]).then_inc(m_freed[i], 1)
                if kind == "w1":
                    e = s[2]
                    i = full(act, ring_m, m_filled, s)
                    if e >= HS:
                        full(act, ring_m, m_filled, ("w2", b, (e - HS) // 2))
                    elif b:
                        full(act, ring_m, m_filled, ("w2", b - 1, E // 2 - 1))
                    nc.scalar.activation(hs[:, e % HS, :], ps_m[i][:, :], ACT.Relu,
                                         bias=b1[:, e:e + 1]).then_inc(m_freed[i], 1)
                    if e == 1:
                        act.wait_ge(routed, ROUTE * b + 2)
                        nc.scalar.activation(ex[:, :, :], lg[:, :, :], ACT.Exp).then_inc(route_exp, 1)
                if kind == "gateT":
                    i = full(act, ring_m, m_filled, s)
                    if b:
                        full(act, ring_m, m_filled, ("gate", b - 1, E // 2 - 1))
                    for dst, done in ((gs[0:E, :], gate_high), (gf[:, :], m_freed[i])):
                        nc.scalar.copy(dst, ps_m[i][0:E, :]).then_inc(done, 1)
                if kind == "gate":
                    i = full(act, ring_m, m_filled, s)
                    if b:
                        act.wait_ge(y_ready, b)
                    nc.scalar.copy(gb[:, s[2], :], ps_m[i][:, :]).then_inc(m_freed[i], 1)

        @block.tensor
        def _(pe):
            def mm(*args, start=True, stop=True):
                return nc.tensor.matmul(*args, start=start, stop=stop)

            def turn(dst, src):
                return nc.tensor.transpose(dst, src, ident[0:src.shape[0], 0:src.shape[0]])

            for s in steps:
                kind, b = s[0], (s[1] if len(s) > 1 else 0)
                if kind == "ffn_setup":
                    i = take(pe, ring_m, m_freed, s)
                    pe.wait_ge(consts, 3 + PARTS + E)
                    pe.wait_ge(ones_ready, 2)
                    pe.wait_ge(halved, 4)
                    for c in range(HC):
                        mm(ps_m[i][0:M, 0:1], w_s2c[:, c, :], ones[:, 0:1], start=(c == 0), stop=(c == HC - 1))
                    for c in range(HC):
                        last = mm(ps_m[i][:, P:P + D], ones[:, :], w_dec[:, c, :], start=(c == 0), stop=(c == HC - 1))
                    last.then_inc(m_filled[i], 1)
                if kind == "xT":
                    i = take(pe, ring_a, a_freed, s)
                    if b == 0:
                        pe.wait_ge(consts, 1)
                    pe.wait_ge(xn_ready, T * (b + 1))
                    for t in range(T):
                        last = turn(ps_a[i][:, P * t:P * t + P], xn[:, t, :])
                    last.then_inc(a_filled[i], 1)
                if kind in ("q", "k"):
                    i = take(pe, ring_a, a_freed, s)
                    if kind == "q":
                        read(pe, ring_a, a_freed, ("xT", b))
                        pe.wait_ge(w_turned, 1)
                    w = w_qk[:, int(kind == "k")].rearrange("p k h -> p (k h)")
                    mm(ps_a[i][:, :], w, xT[:, :]).then_inc(a_filled[i], 1)
                if kind == "v":
                    i = take(pe, ring_a, a_freed, s)
                    pe.wait_ge(qkv_in, 16 * (T + 2))
                    for t in range(T):
                        last = mm(ps_a[i][:, P * t:P * t + P], xT[:, P * t:P * t + P],
                                  wv[:, :, :].rearrange("p h k -> p (h k)"))
                    last.then_inc(a_filled[i], 1)
                if kind == "max":
                    t, h0, nh = MU[s[2]]
                    i = take(pe, ring_a, a_freed, s)
                    for n, first, _ in pieces[b]:
                        if (h0, s[2] % NM) == (first, 0):
                            pe.wait_ge(stacked[n], 16 * STACK_DMAS)
                            pe.wait_ge(rows_set[b % 2], 16 * 3)
                            pe.wait_ge(consts, 3)
                    W = P * (t + 1)
                    for n in range(nh):
                        mm(ps_a[i][:, n * W:n * W + W], qs[b % 2][0:M_ROW, h0 + n, P * t:P * t + P],
                           ks[b % 2][0:M_ROW, h0 + n, 0:W], start=(n == 0), stop=False)
                    dst = ps_a[i][:, 0:nh * W].rearrange("p (n w) -> p n w", n=nh)[:, :, W - P:W]
                    mm(dst, identb[:, :], mask[:, 0:nh, :], start=False).then_inc(a_filled[i], 1)
                if kind == "negmax":
                    _, _, g0, g1 = s
                    i = take(pe, ring_a, a_freed, s)
                    for n in (2, 1):
                        read(pe, ring_a, a_freed, ("max", b, g1 * NM - n))
                    for t in range(T):
                        last = turn(ps_a[i][0:GH * (g1 - g0), P * t:P * t + P], mx[:, t, GH * g0:GH * g1])
                    last.then_inc(a_filled[i], 1)
                if kind == "score":
                    _, _, g, u = s
                    n = (b * G + g) * NS + u
                    if u == 0:
                        for m, k in order_negmax.items():
                            if m[1:3] == (b, g):
                                pe.wait_ge(nm_in[k], 16 * M_PARTS)
                    if n >= 2:
                        pe.wait_ge(probs, n - 1)
                    for h, kt, c in score_parts(u):
                        hh = GH * g + h
                        last = mm(ps_b[n % 2][:, c:c + S - P * kt],
                                  ks[b % 2][0:M_ROW + M_PARTS, hh, P * kt:P * kt + P],
                                  qs[b % 2][0:M_ROW + M_PARTS, hh, P * kt:S])
                    last.then_inc(scores, 1)
                if kind == "pv":
                    _, _, g, c = s
                    kt = (0, 1, 3, 2)[c]
                    half, second = g // 2, g % 2
                    if c == 0:
                        read(pe, ring_a, a_freed, ("v", b))
                        if not second and b:
                            pe.wait_ge(ctx_sb, 2 * (b - 1) + half + 1)
                    pe.wait_ge(masked, (b * G + g) * NS + (4, 8, 8, 10)[c])
                    for j in range(GH):
                        u, off = ((j, 0), (4 + j, 0), (8 + j // 2, 2 * P * (j % 2)), (4 + j, S - P))[kt]
                        w = S - P * kt
                        last = mm(ps_v[half][32 * j:32 * j + 32, P * kt:S], vp[b % 2][:, kt, GH * g + j, :],
                                  pr[:, prob_slot(b, g, u), off:off + w],
                                  start=(not second and c == 0), stop=bool(second and c == NPV - 1))
                    last.then_inc(pv_done, 1)
                if kind == "ctx_tok":
                    i = take(pe, ring_m, m_freed, s)
                    pe.wait_ge(ctx_sb, 2 * b + s[2] + 1)
                    for t in range(T):
                        last = turn(ps_m[i][:, P * t:P * t + P], cu[:, s[2], P * t:P * t + P])
                    last.then_inc(m_filled[i], 1)
                if kind == "ctxT":
                    i = take(pe, ring_m, m_freed, s)
                    for half in range(2):
                        read(pe, ring_m, m_freed, ("ctx_tok", b, half))
                    for t in range(T):
                        last = turn(ps_m[i][:, P * t:P * t + P], ctok[:, t, :])
                    last.then_inc(m_filled[i], 1)
                if kind == "out_proj":
                    i = take(pe, ring_m, m_freed, s)
                    read(pe, ring_m, m_freed, ("ctxT", b))
                    pe.wait_ge(ffn_in, 16 * len(ffn_loads))
                    for t in range(T):
                        last = mm(ps_m[i][:, P * t:P * t + P], dT[:, P * t:P * t + P], wo[:, :])
                    last.then_inc(m_filled[i], 1)
                if kind == "x1T":
                    i = take(pe, ring_m, m_freed, s)
                    pe.wait_ge(xn2_ready, T * (b + 1))
                    for t in range(T):
                        last = turn(ps_m[i][:, P * t:P * t + P], xn2[:, t, :])
                    last.then_inc(m_filled[i], 1)
                if kind == "enc":
                    c = s[2]
                    i = take(pe, ring_m, m_freed, s)
                    read(pe, ring_m, m_freed, ("x1T", b))
                    mm(ps_m[i][:, :], w_enc[:, P * c:P * c + P], dT[:, :]).then_inc(m_filled[i], 1)
                if kind == "s2c":
                    i = take(pe, ring_m, m_freed, s)
                    for c in range(HC):
                        read(pe, ring_m, m_freed, ("enc", b, c))
                        last = mm(ps_m[i][M * c:M * c + M, :], w_s2c[:, c, :], spikes[:, c, :])
                    last.then_inc(m_filled[i], 1)
                if kind == "router":
                    i = take(pe, ring_m, m_freed, s)
                    read(pe, ring_m, m_freed, ("s2c", b))
                    for t in range(T):
                        last = mm(ps_m[i][:, E * t:E * t + E], cont[:, P * t:P * t + P], wr[:, :])
                    last.then_inc(m_filled[i], 1)
                if kind == "w1":
                    i = take(pe, ring_m, m_freed, s)
                    mm(ps_m[i][:, :], w1[:, s[2], :], cont[:, :]).then_inc(m_filled[i], 1)
                if kind == "gateT":
                    i = take(pe, ring_m, m_freed, s)
                    pe.wait_ge(routed, ROUTE * (b + 1))
                    for t in range(T):
                        last = turn(ps_m[i][0:E, P * t:P * t + P], gate[:, t, :])
                    last.then_inc(m_filled[i], 1)
                if kind == "gate":
                    i = take(pe, ring_m, m_freed, s)
                    if s[2] == 0:
                        pe.wait_ge(gate_split, 4 * (b + 1))
                    mm(ps_m[i][:, :], sel[:, s[2], :, :].rearrange("r i m -> r (i m)"), gs[:, :]).then_inc(m_filled[i], 1)
                if kind == "w2":
                    i = take(pe, ring_m, m_freed, s)
                    for n in range(2):
                        e = 2 * s[2] + n
                        read(pe, ring_m, m_freed, ("w1", b, e))
                        last = mm(ps_m[i][M * n:M * n + M, :], w2[:, e, :], hs[:, e % HS, :])
                    last.then_inc(m_filled[i], 1)
                if kind == "c2s":
                    i = take(pe, ring_m, m_freed, s)
                    pe.wait_ge(y_ready, b + 1)
                    mm(ps_m[i][:, :], w_c2s[:, P * s[2]:P * s[2] + P], cont[:, :]).then_inc(m_filled[i], 1)
                if kind == "dec":
                    i = take(pe, ring_m, m_freed, s)
                    for c in range(HC):
                        read(pe, ring_m, m_freed, ("c2s", b, c))
                    for t in range(T):
                        for c in range(HC):
                            last = mm(ps_m[i][:, P * t:P * t + P], spikes[:, c, P * t:P * t + P], w_dec[:, c, :],
                                      start=(c == 0), stop=(c == HC - 1))
                    last.then_inc(m_filled[i], 1)

        @block.vector
        def _(dve):
            def stats(src, st, mv, done, b):
                for t in range(T):
                    nc.vector.bn_stats(st[:, t, :], src[:, t, :]).then_inc(done, 1)
                for t in range(T):
                    dve.wait_ge(done, 2 * T * b + T + t)
                    nc.vector.bn_aggr(mv[:, t, :], st[:, t, :]).then_inc(done, 1)

            def apply_norm(dst, src, mv, rs, done):
                for t in range(T):
                    nc.vector.tensor_scalar(dst[:, t, :], src[:, t, :], mv[:, t, 0:1], rs[:, t:t + 1],
                                            ALU.subtract, ALU.mult).then_inc(done, 1)

            def split2(f, p1, r, p2, p3, done, before):
                if before:
                    dve.wait_ge(done, before)
                nc.vector.tensor_tensor(r, f, p1, ALU.subtract).then_inc(done, 1)
                dve.wait_ge(done, before + 1)
                nc.vector.tensor_copy(p2, r).then_inc(done, 1)
                dve.wait_ge(done, before + 2)
                nc.vector.tensor_tensor(p3, r, p2, ALU.subtract).then_inc(done, 1)

            nc.vector.memset(ones[:, :], 1.0).then_inc(ones_ready, 1)
            nc.vector.memset(gs[:, :], 0.0).then_inc(ones_ready, 1)

            def route(b):
                base = ROUTE * b
                done = [0]

                def wide(x):
                    return x[:, :].unsqueeze(2).to_broadcast([P, T, E])

                def then(ins):
                    ins.then_inc(routed, 1)
                    done[0] += 1
                    dve.wait_ge(routed, base + done[0])

                def tt(dst, x, w, op):
                    then(nc.vector.tensor_tensor(dst[:, :, :], x[:, :, :], w, op))

                def reduce(src, op):
                    then(nc.vector.tensor_reduce(r1[:, :], src[:, :, :], AX_X, op))

                reduce(lg, ALU.max)
                tt(lg, lg, wide(r1), ALU.subtract)
                dve.wait_ge(route_exp, b + 1)
                reduce(ex, ALU.max)
                tt(ra, ex, wide(r1), ALU.is_equal)
                tt(ra, ra, tie_rank[:, :, :], ALU.mult)
                reduce(ra, ALU.max)
                tt(oh1, ra, wide(r1), ALU.is_equal)
                then(nc.vector.scalar_tensor_tensor(out=rb[:, :, :], in0=oh1[:, :, :], scalar=-2.0, in1=ex[:, :, :],
                                                    op0=ALU.mult, op1=ALU.add))
                reduce(rb, ALU.max)
                tt(ra, rb, wide(r1), ALU.is_equal)
                tt(ra, ra, tie_rank[:, :, :], ALU.mult)
                reduce(ra, ALU.max)
                tt(oh2, ra, wide(r1), ALU.is_equal)
                tt(oh1, oh1, oh2[:, :, :], ALU.add)
                tt(ra, ex, oh1[:, :, :], ALU.mult)
                reduce(ra, ALU.add)
                then(nc.vector.reciprocal(r1[:, :], r1[:, :]))
                tt(gate, ra, wide(r1), ALU.mult)
                assert done[0] == ROUTE

            for s in steps:
                kind, b = s[0], (s[1] if len(s) > 1 else 0)
                xb = x_all[:, T * b:T * b + T, :]
                if kind == "stats1":
                    dve.wait_ge(x_in[b], 16)
                    if b:
                        dve.wait_ge(xn_ready, T * b)
                    stats(xb, st1, mv1, ln1, b)
                if kind == "norm1":
                    dve.wait_ge(rstd1, 2 * (b + 1))
                    if b:
                        j, r = bank(ring_a, ("xT", b - 1))
                        dve.wait_ge(a_filled[j], r + 1)
                    apply_norm(xn, xb, mv1, rs1, xn_ready)
                if kind == "norm1" and b == 0:
                    dve.wait_ge(bias_in, 16 * 2 * DK)
                    nc.vector.tensor_scalar(bqs[:, :], bq_raw[:, :], QSCALE, None, ALU.mult).then_inc(bqs_ready, 1)
                if kind in ("q", "k"):
                    w = int(kind == "k")
                    read(dve, ring_a, a_freed, s)
                    dve.wait_ge(qk_high, 2 * b + w + 1)
                    split2(qkf[:, w, :], parts[:, w, 0, :], qkr[:, :], parts[:, w, 1, :], parts[:, w, 2, :],
                           qk_split, SPLIT * b + 3 * w)
                if kind == "v":
                    i = full(dve, ring_a, a_filled, s)
                    if b == 0:
                        dve.wait_ge(vp_ones, 4)
                        dve.wait_ge(qkv_in, 16 * (T + 2))
                    if b >= 2:
                        dve.wait_ge(pv_done, NPV * G * (b - 1))
                    for n in range(2):
                        heads = slice(GH * n, GH * n + GH)
                        src = ps_a[i][:, :].rearrange("p (a h k) -> p a h k", h=2 * GH, k=DK)[:, :, heads, :]
                        bias = bv[:, :, :].rearrange("p t (a h k) -> p (t a) h k", h=2 * GH, k=DK)[:, :, heads, :]
                        dst = vp[b % 2][:, :, :, :].rearrange("p t (a h) w -> p (t a) h w", h=2 * GH)
                        o = nc.vector.tensor_tensor(dst[:, :, heads, SLOT * n:SLOT * n + DK], src, bias, ALU.add)
                    o.then_inc(a_freed[i], 1)
                if kind == "ffn_setup":
                    dve.wait_ge(ffn_in, 16 * len(ffn_loads))
                    nc.vector.tensor_scalar(w_s2c[:, :, :], w_s2c[:, :, :], 0.5, None, ALU.mult).then_inc(halved, 1)
                    nc.vector.tensor_scalar(w_dec[:, :, :], w_dec[:, :, :], 0.5, None, ALU.mult).then_inc(halved, 1)
                    nc.vector.tensor_scalar(b_enc[:, :], b_enc[:, :], 0.5, None, ALU.mult).then_inc(halved, 1)
                    nc.vector.tensor_scalar(b_c2s[:, :], b_c2s[:, :], 0.5, None, ALU.mult).then_inc(halved, 1)
                    i = full(dve, ring_m, m_filled, s)
                    nc.vector.tensor_tensor(b_s2c[0:M, :], b_s2c[0:M, :], ps_m[i][0:M, 0:1], ALU.add
                                            ).then_inc(biases, 1)
                    nc.vector.tensor_tensor(b_dec[:, :], b_dec[:, :], ps_m[i][:, P:P + D], ALU.add
                                            ).then_inc(m_freed[i], 1)
                if kind == "max":
                    t, h0, nh = MU[s[2]]
                    i = full(dve, ring_a, a_filled, s)
                    W = P * (t + 1)
                    src = ps_a[i][:, 0:nh * W].rearrange("p (n w) -> p n w", n=nh)
                    nc.vector.tensor_reduce(mx[:, t, h0:h0 + nh], src, AX_X, ALU.max).then_inc(a_freed[i], 1)
                if kind == "negmax":
                    n = order_negmax[s]
                    heads = slice(0, GH * (s[3] - s[2]))
                    i = full(dve, ring_a, a_filled, s)
                    if n:
                        dve.wait_ge(nm_in[n - 1], 16 * M_PARTS)
                    nc.vector.tensor_copy(nmp[heads, 0, :], ps_a[i][heads, :]).then_inc(nm_split, 1)
                    dve.wait_ge(nm_split, n + 1)
                    nc.vector.tensor_tensor(nmp[heads, 1, :], ps_a[i][heads, :], nmp[heads, 0, :], ALU.subtract
                                            ).then_inc(a_freed[i], 1)
                if kind == "ctx_tok":
                    half = s[2]
                    i = full(dve, ring_m, m_filled, s)
                    v = ps_m[i][:, :].rearrange("p (t j c) -> p t j c", t=T, c=VW)
                    if b or half:
                        read(dve, ring_m, m_freed, ("ctx_tok", b - 1, 1) if half == 0 else ("ctx_tok", b, 0))
                    nc.vector.reciprocal(rsum[:, :, :, :], v[:, :, :, DK:DK + SLOT + 1:SLOT]).then_inc(recip, 1)
                    dve.wait_ge(recip, 2 * b + half + 1)
                    if half == 0 and b:
                        j, r = bank(ring_m, ("ctxT", b - 1))
                        dve.wait_ge(m_filled[j], r + 1)
                    dst = ctok[:, :, :].rearrange("p t (a j k) -> p a t j k", j=GH, k=DK)
                    for n in range(2):
                        o = nc.vector.tensor_tensor(
                            dst[:, 2 * half + n], v[:, :, :, SLOT * n:SLOT * n + DK],
                            rsum[:, :, :, n:n + 1].to_broadcast([P, T, GH, DK]), ALU.mult)
                    o.then_inc(m_freed[i], 1)
                if kind == "out_proj":
                    i = full(dve, ring_m, m_filled, s)
                    dve.wait_ge(x_bo, b + 1)
                    if b:
                        dve.wait_ge(x1_lnb, b)
                    nc.vector.tensor_tensor(x1[:, :, :], ps_m[i][:, :].rearrange("p (t d) -> p t d", t=T),
                                            xb, ALU.add).then_inc(m_freed[i], 1)
                if kind == "stats2":
                    read(dve, ring_m, m_freed, ("out_proj", b))
                    if b:
                        dve.wait_ge(xn2_ready, T * b)
                    stats(x1, st2, mv2, ln2, b)
                if kind == "norm2":
                    if b:
                        dve.wait_ge(res_ready, b)
                    dve.wait_ge(rstd2, 2 * (b + 1))
                    apply_norm(xn2, x1, mv2, rs2, xn2_ready)
                if kind == "router":
                    i = full(dve, ring_m, m_filled, s)
                    nc.vector.tensor_tensor(lg[:, :, :], ps_m[i][:, 0:T * E].rearrange("p (t e) -> p t e", t=T),
                                            br[:, :, :], ALU.add).then_inc(m_freed[i], 1)
                    read(dve, ring_m, m_freed, s)
                    route(b)
                if kind == "gateT":
                    read(dve, ring_m, m_freed, s)
                    dve.wait_ge(gate_high, b + 1)
                    split2(gf[:, :], gs[0:E, :], gr[:, :], g2[:, :], gs[64:64 + E, :], gate_split, 4 * b)
                    nc.vector.tensor_copy(gs[32:32 + E, :], g2[:, :]).then_inc(gate_split, 1)
                if kind == "w2":
                    p_ = s[2]
                    i = full(dve, ring_m, m_filled, s)
                    read(dve, ring_m, m_freed, ("gate", b, p_))
                    nc.vector.scalar_tensor_tensor(out=gb[:, p_, :], in0=ps_m[i][:, :], scalar=b2[:, p_:p_ + 1],
                                                   in1=gb[:, p_, :], op0=ALU.add, op1=ALU.mult
                                                   ).then_inc(m_freed[i], 1)
                    if p_ == E // 2 - 1:
                        for q_ in (p_ - 1, p_):
                            read(dve, ring_m, m_freed, ("w2", b, q_))
                        nc.vector.tensor_tensor(gb[:, 2, :], gb[:, 2, :], gb[:, 3, :], ALU.add).then_inc(w2_sum, 1)
                        dve.wait_ge(w2_sum, b + 1)
                        dve.wait_ge(w2_pool, b + 1)
                        nc.vector.tensor_tensor(cont[:, :], gb[:, 0, :], gb[:, 2, :], ALU.add).then_inc(y_ready, 1)
                if kind == "dec":
                    i = full(dve, ring_m, m_filled, s)
                    if b:
                        dve.wait_ge(stored, 16 * b)
                    nc.vector.tensor_tensor(z[:, :, :], ps_m[i][:, :].rearrange("p (t d) -> p t d", t=T),
                                            b_dec[:, :].unsqueeze(1).to_broadcast([P, T, D]), ALU.add
                                            ).then_inc(m_freed[i], 1)
                    read(dve, ring_m, m_freed, s)
                    if b:
                        dve.wait_ge(zn_ready, T * b)
                    stats(z, st3, mv3, ln3, b)
                if kind == "norm3":
                    dve.wait_ge(rstd3, 2 * (b + 1))
                    apply_norm(xn2, z, mv3, rs3, zn_ready)
                if kind == "result":
                    dve.wait_ge(zn_scaled, b + 1)
                    dve.wait_ge(x1_lnb, b + 1)
                    nc.vector.tensor_tensor(z[:, :, :], xn2[:, :, :], xb, ALU.add).then_inc(res_ready, 1)


_INS = ["L0_attn_embeddings", "L0_attn_Wq", "L0_attn_bq", "L0_attn_Wk", "L0_attn_bk", "L0_attn_Wv", "L0_attn_bv",
        "L0_attn_Wo", "L0_attn_bo", "L0_ffn_W_enc", "L0_ffn_b_enc", "L0_ffn_W_s2c", "L0_ffn_b_s2c", "L0_ffn_Wr",
        "L0_ffn_br", "L0_ffn_W1", "L0_ffn_b1", "L0_ffn_W2", "L0_ffn_b2", "L0_ffn_W_c2s", "L0_ffn_b_c2s",
        "L0_ffn_W_dec", "L0_ffn_b_dec", "L0_ffn_ln_g", "L0_ffn_ln_b"]


def kernel(**inputs):
    import numpy as np
    from concourse import bacc
    from concourse.bass_utils import run_bass_kernel_spmd

    nc = bacc.Bacc("TRN2", target_bir_lowering=False, num_devices=1)
    arrays, aps = {}, {}
    for name in _INS:
        arrays[f"in_{name}"] = np.ascontiguousarray(inputs[name])
        aps[name] = nc.dram_tensor(f"in_{name}", arrays[f"in_{name}"].shape, F32, kind="ExternalInput").ap()
    out = nc.dram_tensor("out", arrays["in_L0_attn_embeddings"].shape, F32, kind="ExternalOutput").ap()
    build(nc, aps, out)
    return run_bass_kernel_spmd(nc, [arrays], core_ids=[0]).results[0]["out"]
```

```python
from contextlib import ExitStack

import concourse.bass as bass
from concourse import mybir

ALU = mybir.AluOpType
ACT = mybir.ActivationFunctionType
F32 = mybir.dt.float32
BF16 = mybir.dt.bfloat16
AX_X = mybir.AxisListType.X

P = 128
EPS = 1e-5
MASKED = -1e30
PARTS = 3
LATE_UNITS = 3
WARM = 12
M_ROW = 96
M_PARTS = 2
A_BANKS, B_BANKS, V_BANKS, M_BANKS = 3, 2, 1, 2


def max_units(heads):
    return [(t, h, n) for t, n in ((1, 2), (0, 4), (3, 1), (2, 1)) for h in range(0, heads, n)]


def score_sets(groups):
    return [(0, g, 0) for g in range(groups)] + [(1, g, pair) for g in range(groups) for pair in range(2)]


def feed_units(B, tiles):
    return [(b, 0, tiles) for b in range(B - 1)] + [(B - 1, 0, tiles // 2), (B - 1, tiles // 2, tiles)]


WINDOWS = {
    "ln": ((-1.388, -1.368), (-2.315, -2.106), (-1.16, -1.062), (-1.156, -1.023)),
    "front": ((-1.324, -0.871), (-1.88, -1.799), (-1.061, -0.888), (-1.069, -0.924)),
    "bo": ((-0.385, -0.385), (-0.452, -0.452), (-0.619, -0.619), (-0.578, -0.578)),
    "maxA": ((-0.637, -0.317), (-0.715, -0.605), (-0.722, -0.506), (-0.766, -0.592)),
    "negA": ((-0.131, -0.131), (-0.222, -0.222), (-0.124, -0.124), (-0.526, -0.526)),
    "maxB": ((-0.141, 0.253), (-0.512, -0.021), (-0.504, 0.106), (-0.577, 0.097)),
    "negB": ((0.271, 0.271), (0.218, 0.218), (0.177, 0.177), (0.225, 0.225)),
    "setsA": ((0.06, 0.29), (0.027, 0.267), (0.006, 0.338), (0.096, 0.283)),
    "setsB": ((0.329, 0.981), (0.33, 1.022), (0.327, 0.97), (0.311, 1.031)),
    "pv_last": ((1.008, 1.008), (1.042, 1.042), (1.044, 1.044), (1.056, 1.056)),
    "ctxA": ((0.378, 0.433), (0.422, 0.485), (0.413, 0.462), (0.395, 0.479)),
    "ctxB": ((1.006, 1.139), (1.023, 1.14), (1.038, 1.141), (1.094, 1.105)),
    "setup": ((0.836, 0.836),),
    "tail": ((1.126, 1.176), (1.136, 1.189), (1.133, 1.172), (0.478, 0.568), (1.141, 1.166)),
    "rstd2": ((1.214, 1.214), (1.214, 1.214), (1.197, 1.197), (0.705, 0.705), (1.224, 1.224)),
    "norm2": ((1.26, 1.26), (1.26, 1.26), (1.256, 1.256), (0.74, 0.74), (1.245, 1.245)),
    "lnb": ((1.617, 1.617), (1.52, 1.52), (1.371, 1.371), (0.786, 0.786), (1.197, 1.197)),
    "enc": ((1.271, 1.419), (1.351, 1.472), (1.274, 1.277), (0.755, 0.836), (1.475, 1.48)),
    "experts": ((1.49, 1.774), (1.507, 1.851), (1.306, 1.605), (0.833, 1.154), (1.551, 1.599)),
    "dec": ((1.878, 1.961), (1.894, 1.926), (1.679, 1.777), (1.298, 1.306), (1.664, 1.761)),
    "rstd3": ((1.963, 1.963), (1.963, 1.963), (1.859, 1.859), (1.341, 1.341), (1.761, 1.761)),
    "norm3": ((2.085, 2.085), (2.085, 2.085), (1.921, 1.921), (1.386, 1.386), (1.898, 1.898)),
    "result": ((2.191, 2.191), (2.147, 2.147), (2.017, 2.017), (1.576, 1.576), (2.612, 2.612)),
}


def schedule(B, heads, groups, tiles):
    placed = []

    def place(part, n, b, steps):
        lo, hi = WINDOWS[part][n]
        for i, s in enumerate(steps):
            placed.append((b + lo + (hi - lo) * (i + 0.5) / len(steps), len(placed), s))

    units = max_units(heads)
    early = sum(1 for t, *_ in units if t < tiles // 2)
    sets = score_sets(groups)
    for b in range(B):
        place("ln", b, b, [("stats1", b), ("norm1", b)])
        place("front", b, b, [(what, b) for what in ("xT", "q", "k", "v")])
        place("bo", b, b, [("add_bo", b)])
        place("maxA", b, b, [("max", b, n) for n in range(early)])
        place("negA", b, b, [("negmax", b, 0)])
        place("maxB", b, b, [("max", b, n) for n in range(early, len(units))])
        place("negB", b, b, [("negmax", b, 1)])
        for half, part in enumerate(("setsA", "setsB")):
            steps = []
            for n, (of, *_) in enumerate(sets):
                if of == half:
                    for h in range(4):
                        steps.append(("score", b, n, h))
                        if n and h == 2:
                            steps.append(("pv", b, n - 1))
            place(part, b, b, steps)
        place("ctxA", b, b, [("ctx_out", b, 0), ("ctx_tok", b, 0)])
        place("pv_last", b, b, [("pv", b, len(sets) - 1)])
        place("ctxB", b, b, [("ctx_out", b, 1), ("ctx_tok", b, 1)])
    place("setup", 0, 0, [("ffn_setup",)])
    for f, (b, *_) in enumerate(feed_units(B, tiles)):
        place("tail", f, b, [(what, f) for what in ("ctxT", "out_proj", "stats2")])
        place("rstd2", f, b, [("rstd2", f)])
        place("norm2", f, b, [("norm2", f)])
        place("lnb", f, b, [("add_lnb", f)])
        place("enc", f, b, [("x1T", f), ("enc", f, 0), ("enc", f, 1), ("s2c", f), ("router", f)])
        w1 = [("w1", f, e) for e in range(8)]
        route = [("route", f, i) for i in range(3)]
        pairs = [(what, f, p) for p in range(4) for what in ("gate", "w2")]
        place("experts", f, b, w1[0:2] + route[0:1] + w1[2:4] + route[1:2] + w1[4:6] + route[2:3] + w1[6:7]
              + [("gateT", f)] + w1[7:8] + pairs)
        place("dec", f, b, [("c2s", f, 0), ("c2s", f, 1), ("dec", f)])
        place("rstd3", f, b, [("rstd3", f)])
        place("norm3", f, b, [("norm3", f)])
        place("result", f, b, [("result", f)])
    return [s for *_, s in sorted(placed)]


def build(nc, a, out):
    B, S, D = a["L0_attn_embeddings"].shape
    H, _, DK = a["L0_attn_Wq"].shape
    HID = a["L0_ffn_W_enc"].shape[1]
    M = a["L0_ffn_W_s2c"].shape[1]
    E, _, EH = a["L0_ffn_W1"].shape
    T = S // P
    HC = HID // P
    GH = 4
    G = H // GH
    SLOTS = 12
    QSCALE = float(DK) ** -0.5
    VW = 32
    SLOT = DK + 1
    HQ = S // 2
    assert (D, EH, S, H * DK, 2 * M, GH, E) == (P, P, 512, P, P, T, 8)

    MU = max_units(H)
    SECOND = MU.index((T - 1, 0, 1))
    SETS = score_sets(G)
    NSET = len(SETS)
    UNITS = feed_units(B, T)
    tiles_before = [sum(t1 - t0 for _, t0, t1 in UNITS[:f]) for f in range(len(UNITS) + 1)]
    diagonal = [half == pair for half, _, pair in SETS]
    steps = list(schedule(B, H, G, T))

    def in_ring_a(s):
        return (s[0] in ("xT", "q", "k", "v", "max", "negmax")
                or s[0] in ("w1", "gate") and s[1] >= len(UNITS) - LATE_UNITS)

    ring_a = {s: n for n, s in enumerate([s for s in steps if in_ring_a(s)])}
    ring_m = {s: n for n, s in enumerate([s for s in steps if not in_ring_a(s) and s[0] in (
        "ffn_setup", "ctx_tok", "ctxT", "out_proj", "x1T", "enc", "s2c", "router", "w1", "gateT", "gate", "w2",
        "c2s", "dec")])}
    order_negmax = {s: n for n, s in enumerate([s for s in steps if s[0] == "negmax"])}

    with ExitStack() as ctx:
        def sb(name, shape, dt=F32):
            return ctx.enter_context(nc.sbuf_tensor(name, shape, dt))

        def sem(name):
            return ctx.enter_context(nc.semaphore(name))

        def banks(name, n):
            return [ctx.enter_context(nc.psum_tensor(f"{name}{i}", [P, 512], F32)) for i in range(n)]

        ps_a = banks("ps_a", A_BANKS)
        ps_b = banks("ps_b", B_BANKS)
        ps_v = banks("ps_v", V_BANKS)
        ps_m = banks("ps_m", M_BANKS)

        ident = sb("ident", [P, P])
        identb = sb("identb", [P, P], BF16)
        mask = sb("mask", [P, 4, P], BF16)
        ones = sb("ones", [P, P])
        minus_half = sb("minus_half", [P, T])
        tie_rank = sb("tie_rank", [P, T, E])
        sel = sb("sel", [M_ROW, E // 2, 2, M], BF16)
        x_all = sb("x_all", [P, B * T, D])
        w_qk_raw = sb("w_qk_raw", [P, 2, H, DK])
        w_qk = sb("w_qk", [P, 2, DK, H])
        wv = sb("wv", [P, H, DK])
        bq_raw = sb("bq_raw", [P, 1])
        bqs = sb("bqs", [P, 1])
        bk = sb("bk", [P, 1])
        bv = sb("bv", [P, T, H * DK])
        wo = sb("wo", [P, D])
        bo = sb("bo", [P, D])
        w_enc = sb("w_enc", [P, HID])
        b_enc = sb("b_enc", [P, HC])
        w_s2c = sb("w_s2c", [P, HC, M])
        b_s2c = sb("b_s2c", [P, 1])
        wr = sb("wr", [P, E])
        br = sb("br", [P, T, E])
        zeros_b = sb("zeros_b", [M_ROW - PARTS * PARTS * DK, S], BF16)
        minus_b = sb("minus_b", [M_PARTS, S], BF16)
        w1 = sb("w1", [P, E, EH])
        b1 = sb("b1", [P, E])
        w2 = sb("w2", [P, E, M])
        b2 = sb("b2", [P, E // 2])
        w_c2s = sb("w_c2s", [P, HID])
        b_c2s = sb("b_c2s", [P, HC])
        w_dec = sb("w_dec", [P, HC, D])
        b_dec = sb("b_dec", [P, D])
        ln_g = sb("ln_g", [P, D])
        ln_b = sb("ln_b", [P, D])

        st1 = sb("st1", [P, T, 6])
        mv1 = sb("mv1", [P, T, 2])
        rs1 = sb("rs1", [P, T])
        xn = sb("xn", [P, T, D])
        xT = sb("xT", [P, S])
        qkf = sb("qkf", [P, 2, S])
        qkr = sb("qkr", [P, S])
        parts = sb("parts", [P, 2, PARTS, S], BF16)
        qs = [sb(f"qs{i}", [P, H, S], BF16) for i in range(2)]
        ks = [sb(f"ks{i}", [P, H, S], BF16) for i in range(2)]
        vp = [sb(f"vp{i}", [P, T, H, VW]) for i in range(2)]
        mx = sb("mx", [P, T, H])
        nmp = sb("nmp", [H, M_PARTS, S], BF16)
        pr = sb("pr", [P, SLOTS, S])
        cu = sb("cu", [P, 2, S])
        rsum = sb("rsum", [P, T, GH, 2])
        ctok = sb("ctok", [P, T, H * DK])
        cT = sb("cT", [P, S])

        x1 = sb("x1", [P, T, D])
        st2 = sb("st2", [P, T, 6])
        mv2 = sb("mv2", [P, T, 2])
        rs2 = sb("rs2", [P, T])
        xn2 = sb("xn2", [P, T, D])
        x1T = sb("x1T", [P, S])
        spikes = sb("spikes", [P, HC, S])
        cont = sb("cont", [P, S])
        lg = sb("lg", [P, T, E])
        ex = sb("ex", [P, T, E])
        ra = sb("ra", [P, T, E])
        rb = sb("rb", [P, T, E])
        oh1 = sb("oh1", [P, T, E])
        oh2 = sb("oh2", [P, T, E])
        r1 = sb("r1", [P, T])
        gate = sb("gate", [P, T, E])
        gf = sb("gf", [E, S])
        gr = sb("gr", [E, S])
        g2 = sb("g2", [E, S], BF16)
        gs = sb("gs", [M_ROW, S], BF16)
        hs = sb("hs", [P, E, S])
        gb = sb("gb", [P, E // 2, S])
        z = sb("z", [P, T, D])
        st3 = sb("st3", [P, T, 6])
        mv3 = sb("mv3", [P, T, 2])
        rs3 = sb("rs3", [P, T])

        x_in = [sem(f"x_in{b}") for b in range(B)]
        w_qk_in = sem("w_qk_in")
        qkv_in = sem("qkv_in")
        ffn_in = sem("ffn_in")
        filled = sem("filled")
        consts = sem("consts")
        vp_ones = sem("vp_ones")
        rows_set = [sem(f"rows_set{i}") for i in range(2)]
        tiles_set = sem("tiles_set")
        bias_in = sem("bias_in")
        bqs_ready = sem("bqs_ready")
        w_turned = sem("w_turned")
        halved = sem("halved")
        a_filled = [sem(f"a_filled{i}") for i in range(A_BANKS)]
        a_freed = [sem(f"a_freed{i}") for i in range(A_BANKS)]
        m_filled = [sem(f"m_filled{i}") for i in range(M_BANKS)]
        m_freed = [sem(f"m_freed{i}") for i in range(M_BANKS)]
        ln1 = sem("ln1")
        rstd1 = sem("rstd1")
        xn_ready = sem("xn_ready")
        x_bo = sem("x_bo")
        qk_high = sem("qk_high")
        qk_split = sem("qk_split")
        gate_high = sem("gate_high")
        in_dram = [[sem(f"in_dram{b}{w}") for w in "qk"] for b in range(B)]
        stacked = [sem(f"stacked{i}") for i in range(B + 1)]
        nm_split = sem("nm_split")
        nm_in = [sem(f"nm_in{i}") for i in range(len(order_negmax))]
        scores = sem("scores")
        probs = sem("probs")
        masked = sem("masked")
        pv_done = sem("pv_done")
        ctx_sb = sem("ctx_sb")
        recip = sem("recip")
        ln2 = sem("ln2")
        rstd2 = sem("rstd2")
        xn2_ready = sem("xn2_ready")
        x1_lnb = sem("x1_lnb")
        routed = sem("routed")
        route_exp = sem("route_exp")
        gate_split = sem("gate_split")
        w2_pool = sem("w2_pool")
        w2_sum = sem("w2_sum")
        y_ready = sem("y_ready")
        ln3 = sem("ln3")
        rstd3 = sem("rstd3")
        zn_ready = sem("zn_ready")
        zn_scaled = sem("zn_scaled")
        res_ready = sem("res_ready")
        stored = sem("stored")

        SPLIT = 6
        ROUTE = 18

        parts_dram = nc.dram_tensor("parts_dram", [B, 2, PARTS, P * S], BF16, kind="Internal").ap()
        pieces = [[(0, 0, HQ), (1, HQ, S)]] + [[(b + 1, 0, S)] for b in range(1, B)]
        STACK_DMAS = 1 + PARTS

        def bank(ring, s):
            n, size = ring[s], A_BANKS if ring is ring_a else M_BANKS
            return n % size, n // size

        def take(eng, ring, freed, s):
            i, r = bank(ring, s)
            if r:
                eng.wait_ge(freed[i], r)
            return i

        def read(eng, ring, freed, s):
            i, r = bank(ring, s)
            eng.wait_ge(freed[i], r + 1)

        def full(eng, ring, filled, s):
            i, r = bank(ring, s)
            eng.wait_ge(filled[i], r + 1)
            return i

        def home(s):
            return (ring_a, ps_a, a_filled, a_freed) if s in ring_a else (ring_m, ps_m, m_filled, m_freed)

        def span(s):
            if s[0] not in ("ctxT", "out_proj", "stats2", "rstd2", "norm2", "add_lnb", "x1T", "enc", "s2c", "router",
                            "w1", "route", "gateT", "gate", "w2", "c2s", "dec", "rstd3", "norm3", "result"):
                return (s[1] if len(s) > 1 else 0), 0, 0, T
            b, t0, t1 = UNITS[s[1]]
            return b, s[1], t0, t1

        def score_parts(n):
            half, _, pair = SETS[n]
            parts_ = []
            for i in range(2):
                kt = 2 * pair + i
                q0 = max(P * kt, HQ * half)
                parts_.append((kt, HQ * i, q0, HQ * (half + 1) - q0))
            return parts_

        def prob_slot(b, n, h):
            return ((b * NSET + n) * GH + h) % SLOTS

        def diagonals(b, n):
            return b * sum(diagonal) + sum(diagonal[:n + 1])

        block = ctx.enter_context(nc.Block())

        def rows(x):
            return x.partition_broadcast(P)

        ffn_loads = [
            (w_s2c[:, :, :], a["L0_ffn_W_s2c"].rearrange("(c p) m -> p c m", p=P)),
            (b_s2c[0:M, :], a["L0_ffn_b_s2c"].unsqueeze(1)),
            (w_dec[:, :, :], a["L0_ffn_W_dec"].rearrange("(c p) d -> p c d", p=P)),
            (b_dec[:, :], rows(a["L0_ffn_b_dec"])),
            (b_enc[:, :], a["L0_ffn_b_enc"].rearrange("(c p) -> p c", p=P)),
            (b_c2s[:, :], a["L0_ffn_b_c2s"].rearrange("(c p) -> p c", p=P)),
            (wo[:, :], a["L0_attn_Wo"]),
            (w_enc[:, :], a["L0_ffn_W_enc"]),
            (b1[:, :], a["L0_ffn_b1"].rearrange("e h -> h e")),
            (w2[:, :, :], a["L0_ffn_W2"].rearrange("e h m -> h e m")),
            (ln_g[:, :], rows(a["L0_ffn_ln_g"])),
            (ln_b[:, :], rows(a["L0_ffn_ln_b"])),
        ]
        ffn_loads.append((br[:, :, :], rows(a["L0_ffn_br"]).unsqueeze(1).to_broadcast([P, T, E])))
        for i in range(2):
            half = slice(M * i, M * i + M)
            ffn_loads += [
                (wr[half, :], a["L0_ffn_Wr"]),
                (w1[half, :, :], a["L0_ffn_W1"].rearrange("e m h -> m e h")),
                (w_c2s[half, :], a["L0_ffn_W_c2s"]),
                (b2[half, :], a["L0_ffn_b2"].rearrange("(p i) m -> i m p", i=2)[i]),
            ]

        @block.sync
        def _(sp):
            x_dram = a["L0_attn_embeddings"].rearrange("b (t p) d -> p b t d", p=P)
            with nc.allow_non_contiguous_dma(reason="small transposed biases"):
                sp.dma_start(x_all[:, 0:T, :], x_dram[:, 0]).then_inc(x_in[0], 16)
                sp.dma_start(w_qk_raw[:, 1], a["L0_attn_Wk"].rearrange("h d k -> d h k")).then_inc(w_qk_in, 16)
                sp.dma_start(wv[:, :, :], a["L0_attn_Wv"].rearrange("h d k -> d h k")).then_inc(qkv_in, 16)
                sp.dma_start(bv[:, :, :], rows(a["L0_attn_bv"].rearrange("h k -> (h k)")).unsqueeze(1)
                             .to_broadcast([P, T, H * DK])).then_inc(qkv_in, 16)
                sp.dma_start(bo[:, :], rows(a["L0_attn_bo"])).then_inc(qkv_in, 16)
                sp.dma_start(x_all[:, T:2 * T, :], x_dram[:, 1]).then_inc(x_in[1], 16)
            sp.wait_ge(filled, 3)
            r0 = PARTS * PARTS * DK

            def constant_rows(i):
                for st in (qs[i], ks[i]):
                    sp.dma_start(st[r0:M_ROW, :, :], zeros_b[:, :].unsqueeze(1).to_broadcast([M_ROW - r0, H, S])
                                 ).then_inc(rows_set[i], 16)
                sp.dma_start(ks[i][M_ROW:M_ROW + M_PARTS, :, :],
                             minus_b[:, :].unsqueeze(1).to_broadcast([M_PARTS, H, S])).then_inc(rows_set[i], 16)

            constant_rows(0)
            for s in steps:
                if s[0] in ("q", "k"):
                    b, w = s[1], int(s[0] == "k")
                    sp.wait_ge(qk_split, SPLIT * b + 3 * (w + 1))
                    sp.dma_start(parts_dram[b, w].rearrange("i (p t) -> p i t", p=P), parts[:, w, :, :]
                                 ).then_inc(in_dram[b][w], 16)
                if s[0] == "k":
                    sp.wait_ge(in_dram[b][0], 16)
                    if b >= 2:
                        sp.wait_ge(pv_done, NSET * (b - 1))
                    for n, c0, c1 in pieces[b]:
                        src = parts_dram[b, 0].rearrange("i (d h t) -> (i d) h t", d=DK, h=H)[:, :, c0:c1]
                        sp.dma_start(qs[b % 2][0:r0, :, c0:c1],
                                     src.unsqueeze(0).to_broadcast([PARTS, PARTS * DK, H, c1 - c0])
                                     ).then_inc(stacked[n], 16)
                        if c0 == 0:
                            sp.wait_ge(in_dram[b][1], 16)
                        for i in range(PARTS):
                            src = parts_dram[b, 1, i].rearrange("(d h t) -> d h t", d=DK, h=H)[:, :, c0:c1]
                            sp.dma_start(ks[b % 2][PARTS * DK * i:PARTS * DK * (i + 1), :, c0:c1],
                                         src.unsqueeze(0).to_broadcast([PARTS, DK, H, c1 - c0])
                                         ).then_inc(stacked[n], 16)
                    if b == 0:
                        for n in range(2, B):
                            sp.dma_start(x_all[:, T * n:T * n + T, :], x_dram[:, n]).then_inc(x_in[n], 16)
                        constant_rows(1)
                if s[0] == "negmax":
                    _, b, half = s
                    n = order_negmax[s]
                    read(sp, ring_a, a_freed, s)
                    for part in range(M_PARTS):
                        sp.dma_start(qs[b % 2][M_ROW + part:M_ROW + part + 1, :, HQ * half:HQ * half + HQ],
                                     nmp[:, part, HQ * half:HQ * half + HQ]).then_inc(nm_in[n], 16)
                    if n < 2:
                        half = len(ffn_loads) // 2
                        sp.wait_ge(filled, 4)
                        with nc.allow_non_contiguous_dma(reason="small transposed biases"):
                            for dst, src in (ffn_loads[half:] if n else ffn_loads[:half]):
                                sp.dma_start(dst, src).then_inc(ffn_in, 16)
                if s[0] == "result":
                    b, t0, t1 = UNITS[s[1]]
                    sp.wait_ge(res_ready, s[1] + 1)
                    sp.dma_start(out.rearrange("b (t p) d -> p b t d", p=P)[:, b, t0:t1], z[:, t0:t1, :]
                                 ).then_inc(stored, 16)
            sp.wait_ge(stored, 16 * len(UNITS))

        @block.gpsimd
        def _(pool):
            nc.gpsimd.memset(minus_half[:, :], -0.5).then_inc(filled, 1)
            nc.gpsimd.memset(zeros_b[:, :], 0.0).then_inc(filled, 1)
            nc.gpsimd.memset(minus_b[:, :], -1.0).then_inc(filled, 1)
            nc.gpsimd.memset(b_s2c[:, :], 0.0).then_inc(filled, 1)
            for t_ in (ident, identb, mask):
                nc.gpsimd.memset(t_[:], 0.0).then_inc(filled, 1)
            pool.wait_ge(filled, 7)
            nc.gpsimd.affine_select(out=ident[:, :], in_=ident[:, :], compare_op=ALU.not_equal, fill=1.0, base=0,
                                    pattern=[[-1, P]], channel_multiplier=1).then_inc(consts, 1)

            def masks():
                nc.gpsimd.affine_select(out=identb[:, :], in_=identb[:, :], compare_op=ALU.not_equal, fill=1.0,
                                        base=0, pattern=[[-1, P]], channel_multiplier=1).then_inc(consts, 1)
                nc.gpsimd.affine_select(out=mask[:, :, :], in_=mask[:, :, :], compare_op=ALU.is_ge, fill=MASKED,
                                        base=0, pattern=[[0, 4], [-1, P]], channel_multiplier=1).then_inc(consts, 1)

            def padded_values():
                for n in range(2):
                    nc.gpsimd.memset(vp[n][:, :, :, :], 0.0).then_inc(filled, 1)
                pool.wait_ge(filled, 9)
                for n in range(2):
                    for second in range(2):
                        v = vp[n][:, :, :, :].rearrange("p t (a h) w -> p (t a) h w", h=2 * GH)
                        c = SLOT * second + DK
                        nc.gpsimd.memset(v[:, :, GH * second:GH * second + GH, c:c + 1], 1.0).then_inc(vp_ones, 1)

            def selectors():
                nc.gpsimd.memset(sel[:, :, :, :], 0.0).then_inc(filled, 1)
                pool.wait_ge(filled, 10)
                for i in range(PARTS):
                    v = sel[32 * i:32 * i + 32, :, :, :].rearrange("r p i m -> r (p i) m")
                    nc.gpsimd.affine_select(out=v, in_=v, compare_op=ALU.not_equal, fill=1.0, base=0,
                                            pattern=[[-1, E], [0, M]], channel_multiplier=1).then_inc(consts, 1)
                    pool.wait_ge(consts, 4 + i)
                for e in range(E):
                    nc.gpsimd.memset(tie_rank[:, :, e:e + 1], float(E - e)).then_inc(consts, 1)

            for s in steps:
                kind = s[0]
                b, f, t0, t1 = span(s)
                tl, cols = slice(t0, t1), slice(P * t0, P * t1)
                if kind in ("stats1", "rstd2", "rstd3"):
                    stats, rstd, mv, rs = {"stats1": (ln1, rstd1, mv1, rs1), "rstd2": (ln2, rstd2, mv2, rs2),
                                           "rstd3": (ln3, rstd3, mv3, rs3)}[kind]
                    n, tiles = (b, T * (b + 1)) if kind == "stats1" else (f, tiles_before[f + 1])
                    pool.wait_ge(stats, 2 * tiles)
                    nc.gpsimd.tensor_scalar(rs[:, tl], mv[:, tl, 1], EPS, None, ALU.add).then_inc(rstd, 1)
                    pool.wait_ge(rstd, 2 * n + 1)
                    nc.gpsimd.tensor_tensor(rs[:, tl], rs[:, tl], minus_half[:, tl], ALU.pow).then_inc(rstd, 1)
                if kind == "stats1" and b == 0:
                    masks()
                    padded_values()
                if kind == "negmax" and order_negmax[s] == 0:
                    selectors()
                if kind == "add_bo":
                    pool.wait_ge(xn_ready, T * (b + 1))
                    pool.wait_ge(qkv_in, 16 * 3)
                    xb = x_all[:, T * b:T * b + T, :]
                    nc.gpsimd.tensor_tensor(xb, xb, bo[:, :].unsqueeze(1).to_broadcast([P, T, D]),
                                            ALU.add).then_inc(x_bo, 1)
                if kind == "score" and diagonal[s[2]]:
                    _, _, n, h = s
                    pool.wait_ge(probs, (b * NSET + n) * GH + h + 1)
                    v = pr[:, prob_slot(b, n, h), :].rearrange("p (a c) -> p a c", a=2)[:, :, 0:P]
                    nc.gpsimd.affine_select(out=v, in_=v, compare_op=ALU.is_ge, fill=0.0, base=0,
                                            pattern=[[0, 2], [1, P]], channel_multiplier=-1).then_inc(masked, 1)
                if kind == "add_lnb":
                    pool.wait_ge(ffn_in, 16 * len(ffn_loads))
                    read(pool, ring_m, m_freed, ("out_proj", f))
                    nc.gpsimd.tensor_tensor(x_all[:, T * b + t0:T * b + t1, :], x1[:, tl, :],
                                            ln_b[:, :].unsqueeze(1).to_broadcast([P, t1 - t0, D]),
                                            ALU.add).then_inc(x1_lnb, 1)
                if kind == "w2" and s[2] == 1:
                    for p_ in range(2):
                        read(pool, ring_m, m_freed, ("w2", f, p_))
                    nc.gpsimd.tensor_tensor(gb[:, 0, cols], gb[:, 0, cols], gb[:, 1, cols], ALU.add
                                            ).then_inc(w2_pool, 1)
                if kind == "norm3":
                    pool.wait_ge(zn_ready, tiles_before[f + 1])
                    nc.gpsimd.tensor_tensor(z[:, tl, :], z[:, tl, :],
                                            ln_g[:, :].unsqueeze(1).to_broadcast([P, t1 - t0, D]),
                                            ALU.mult).then_inc(zn_scaled, 1)

        @block.scalar
        def _(act):
            with nc.allow_non_contiguous_dma(reason="small transposed biases"):
                act.dma_start(w_qk_raw[:, 0], a["L0_attn_Wq"].rearrange("h d k -> d h k")).then_inc(w_qk_in, 16)
                for dst, name in ((bq_raw, "bq"), (bk, "bk")):
                    act.dma_start(dst[:, :], a[f"L0_attn_{name}"].rearrange("h (k o) -> k h o", o=1)
                                  ).then_inc(bias_in, 16)
            act.wait_ge(w_qk_in, 32)
            nc.scalar.copy(w_qk[:, :, :, :], w_qk_raw[:, :, :, :].rearrange("p w h k -> p w k h")).then_inc(w_turned, 1)

            for s in steps:
                kind = s[0]
                b, f, t0, t1 = span(s)
                tl, cols = slice(t0, t1), slice(P * t0, P * t1)
                if kind == "xT":
                    i = full(act, ring_a, a_filled, s)
                    if b:
                        j, r = bank(ring_a, ("v", b - 1))
                        act.wait_ge(a_filled[j], r + 1)
                    nc.scalar.copy(xT[:, :], ps_a[i][:, :]).then_inc(a_freed[i], 1)
                if kind in ("q", "k"):
                    w = int(kind == "k")
                    i = full(act, ring_a, a_filled, s)
                    act.wait_ge(bqs_ready, 1)
                    if b:
                        act.wait_ge(in_dram[b - 1][w], 16)
                    for dst, done in ((parts[:, w, 0, :], qk_high), (qkf[:, w, :], a_freed[i])):
                        nc.scalar.activation(dst, ps_a[i][:, :], ACT.Identity, bias=(bk if w else bqs)[:, 0:1],
                                             scale=1.0 if w else QSCALE).then_inc(done, 1)
                if kind == "score":
                    _, _, n, h = s
                    m = (b * NSET + n) * GH + h
                    act.wait_ge(scores, m + 1)
                    if m >= SLOTS:
                        act.wait_ge(pv_done, (m - SLOTS) // GH + 1)
                    w = HQ + P if diagonal[n] else S
                    nc.scalar.activation(pr[:, prob_slot(b, n, h), 0:w], ps_b[m % B_BANKS][:, 0:w],
                                         ACT.Exp).then_inc(probs, 1)
                if kind == "ctx_out":
                    half = s[2]
                    act.wait_ge(pv_done, NSET * b + (NSET if half else G))
                    if b:
                        j, r = bank(ring_m, ("ctx_tok", b - 1, half))
                        act.wait_ge(m_filled[j], r + 1)
                    nc.scalar.copy(cu[:, half, :], ps_v[(2 * b + half) % V_BANKS][:, :]).then_inc(ctx_sb, 1)
                if kind in ("ctxT", "x1T"):
                    i = full(act, ring_m, m_filled, s)
                    dst = cT if kind == "ctxT" else x1T
                    nc.scalar.copy(dst[:, cols], ps_m[i][:, cols]).then_inc(m_freed[i], 1)
                if kind in ("enc", "c2s"):
                    c = s[2]
                    if f == 0 and c == 0:
                        read(act, ring_m, m_freed, ("ffn_setup",))
                    i = full(act, ring_m, m_filled, s)
                    bias = b_enc if kind == "enc" else b_c2s
                    nc.scalar.activation(spikes[:, c, cols], ps_m[i][:, cols], ACT.Tanh, bias=bias[:, c:c + 1],
                                         scale=0.5).then_inc(m_freed[i], 1)
                if kind == "s2c":
                    i = full(act, ring_m, m_filled, s)
                    nc.scalar.activation(cont[:, cols], ps_m[i][:, cols], ACT.Identity,
                                         bias=b_s2c[:, 0:1]).then_inc(m_freed[i], 1)
                if kind == "w1":
                    e = s[2]
                    ring, ps, filled_, freed = home(s)
                    i = full(act, ring, filled_, s)
                    if f and t0 == 0:
                        full(act, ring_m, m_filled, ("w2", f - 1, e // 2))
                    nc.scalar.activation(hs[:, e, cols], ps[i][:, cols], ACT.Relu,
                                         bias=b1[:, e:e + 1]).then_inc(freed[i], 1)
                    if e == 1:
                        act.wait_ge(routed, ROUTE * f + 2)
                        nc.scalar.activation(ex[:, tl, :], lg[:, tl, :], ACT.Exp).then_inc(route_exp, 1)
                if kind == "gateT":
                    i = full(act, ring_m, m_filled, s)
                    if f and t0 == 0:
                        before = ("gate", f - 1, E // 2 - 1)
                        full(act, home(before)[0], home(before)[2], before)
                    for dst, done in ((gs[0:E, cols], gate_high), (gf[:, cols], m_freed[i])):
                        nc.scalar.copy(dst, ps_m[i][0:E, cols]).then_inc(done, 1)
                if kind == "gate":
                    ring, ps, filled_, freed = home(s)
                    i = full(act, ring, filled_, s)
                    if f and t0 == 0:
                        act.wait_ge(y_ready, f)
                    nc.scalar.copy(gb[:, s[2], cols], ps[i][:, cols]).then_inc(freed[i], 1)

        @block.tensor
        def _(pe):
            def mm(*args, start=True, stop=True):
                return nc.tensor.matmul(*args, start=start, stop=stop)

            def turn(dst, src):
                return nc.tensor.transpose(dst, src, ident[0:src.shape[0], 0:src.shape[0]])

            pe.wait_ge(tiles_set, 1)
            for _ in range(WARM):
                mm(ps_m[0][:, 0:P], ones[:, :], ones[:, :])

            for s in steps:
                kind = s[0]
                b, f, t0, t1 = span(s)
                tl, cols = slice(t0, t1), slice(P * t0, P * t1)
                if kind == "ffn_setup":
                    i = take(pe, ring_m, m_freed, s)
                    pe.wait_ge(consts, 3 + PARTS + E)
                    pe.wait_ge(tiles_set, 2)
                    pe.wait_ge(halved, 4)
                    for c in range(HC):
                        mm(ps_m[i][0:M, 0:1], w_s2c[:, c, :], ones[:, 0:1], start=(c == 0), stop=(c == HC - 1))
                    for c in range(HC):
                        last = mm(ps_m[i][:, P:P + D], ones[:, :], w_dec[:, c, :], start=(c == 0), stop=(c == HC - 1))
                    last.then_inc(m_filled[i], 1)
                if kind == "xT":
                    i = take(pe, ring_a, a_freed, s)
                    if b == 0:
                        pe.wait_ge(consts, 1)
                    pe.wait_ge(xn_ready, T * (b + 1))
                    for t in range(T):
                        last = turn(ps_a[i][:, P * t:P * t + P], xn[:, t, :])
                    last.then_inc(a_filled[i], 1)
                if kind in ("q", "k"):
                    i = take(pe, ring_a, a_freed, s)
                    if kind == "q":
                        read(pe, ring_a, a_freed, ("xT", b))
                        pe.wait_ge(w_turned, 1)
                    w = w_qk[:, int(kind == "k")].rearrange("p k h -> p (k h)")
                    mm(ps_a[i][:, :], w, xT[:, :]).then_inc(a_filled[i], 1)
                if kind == "v":
                    i = take(pe, ring_a, a_freed, s)
                    pe.wait_ge(qkv_in, 16 * 3)
                    for t in range(T):
                        last = mm(ps_a[i][:, P * t:P * t + P], xT[:, P * t:P * t + P],
                                  wv[:, :, :].rearrange("p h k -> p (h k)"))
                    last.then_inc(a_filled[i], 1)
                if kind == "max":
                    t, h0, nh = MU[s[2]]
                    i = take(pe, ring_a, a_freed, s)
                    for n, first, _ in pieces[b]:
                        if s[2] == (SECOND if first else 0):
                            pe.wait_ge(stacked[n], 16 * STACK_DMAS)
                            pe.wait_ge(rows_set[b % 2], 16 * 3)
                            pe.wait_ge(consts, 3)
                    W = P * (t + 1)
                    for n in range(nh):
                        mm(ps_a[i][:, n * W:n * W + W], qs[b % 2][0:M_ROW, h0 + n, P * t:P * t + P],
                           ks[b % 2][0:M_ROW, h0 + n, 0:W], start=(n == 0), stop=False)
                    dst = ps_a[i][:, 0:nh * W].rearrange("p (n w) -> p n w", n=nh)[:, :, W - P:W]
                    mm(dst, identb[:, :], mask[:, 0:nh, :], start=False).then_inc(a_filled[i], 1)
                if kind == "negmax":
                    half = s[2]
                    i = take(pe, ring_a, a_freed, s)
                    own = [("max", b, n) for n in range(len(MU)) if MU[n][0] // 2 == half]
                    for j in range(A_BANKS):
                        read(pe, ring_a, a_freed, [m for m in own if bank(ring_a, m)[0] == j][-1])
                    for t in range(2):
                        last = turn(ps_a[i][0:H, P * t:P * t + P], mx[:, 2 * half + t, :])
                    last.then_inc(a_filled[i], 1)
                if kind == "score":
                    _, _, n, h = s
                    m = (b * NSET + n) * GH + h
                    half, g, _ = SETS[n]
                    if h == 0 and n in (0, G):
                        pe.wait_ge(nm_in[order_negmax[("negmax", b, half)]], 16 * M_PARTS)
                    if m >= B_BANKS:
                        pe.wait_ge(probs, m - B_BANKS + 1)
                    for kt, c, q0, w in score_parts(n):
                        last = mm(ps_b[m % B_BANKS][:, c:c + w],
                                  ks[b % 2][0:M_ROW + M_PARTS, GH * g + h, P * kt:P * kt + P],
                                  qs[b % 2][0:M_ROW + M_PARTS, GH * g + h, q0:q0 + w])
                    last.then_inc(scores, 1)
                if kind == "pv":
                    n = s[2]
                    half, g, _ = SETS[n]
                    if n == 0:
                        read(pe, ring_a, a_freed, ("v", b))
                    if n in (0, G) and 2 * b + half >= V_BANKS:
                        pe.wait_ge(ctx_sb, 2 * b + half + 1 - V_BANKS)
                    if diagonal[n]:
                        pe.wait_ge(masked, GH * diagonals(b, n))
                    else:
                        pe.wait_ge(probs, GH * (b * NSET + n + 1))
                    for kt, c, q0, w in score_parts(n):
                        for j in range(GH):
                            x = HQ * (g // 2) + q0 - HQ * half
                            last = mm(ps_v[(2 * b + half) % V_BANKS][32 * j:32 * j + 32, x:x + w],
                                      vp[b % 2][:, kt, GH * g + j, :], pr[:, prob_slot(b, n, j), c:c + w],
                                      start=(g % 2 == 0 and kt == 0), stop=(g % 2 == 1 and kt == 2 * half + 1))
                    last.then_inc(pv_done, 1)
                if kind == "ctx_tok":
                    i = take(pe, ring_m, m_freed, s)
                    pe.wait_ge(ctx_sb, 2 * b + s[2] + 1)
                    for t in range(2):
                        for pair in range(2):
                            last = turn(ps_m[i][:, P * (2 * t + pair):P * (2 * t + pair) + P],
                                        cu[:, s[2], HQ * pair + P * t:HQ * pair + P * t + P])
                    last.then_inc(m_filled[i], 1)
                if kind == "ctxT":
                    i = take(pe, ring_m, m_freed, s)
                    for half in range(t0 // 2, t1 // 2):
                        read(pe, ring_m, m_freed, ("ctx_tok", b, half))
                    for t in range(t0, t1):
                        last = turn(ps_m[i][:, P * t:P * t + P], ctok[:, t, :])
                    last.then_inc(m_filled[i], 1)
                if kind == "out_proj":
                    i = take(pe, ring_m, m_freed, s)
                    read(pe, ring_m, m_freed, ("ctxT", f))
                    pe.wait_ge(ffn_in, 16 * len(ffn_loads))
                    for t in range(t0, t1):
                        last = mm(ps_m[i][:, P * t:P * t + P], cT[:, P * t:P * t + P], wo[:, :])
                    last.then_inc(m_filled[i], 1)
                if kind == "x1T":
                    i = take(pe, ring_m, m_freed, s)
                    pe.wait_ge(xn2_ready, tiles_before[f + 1])
                    for t in range(t0, t1):
                        last = turn(ps_m[i][:, P * t:P * t + P], xn2[:, t, :])
                    last.then_inc(m_filled[i], 1)
                if kind == "enc":
                    c = s[2]
                    i = take(pe, ring_m, m_freed, s)
                    read(pe, ring_m, m_freed, ("x1T", f))
                    mm(ps_m[i][:, cols], w_enc[:, P * c:P * c + P], x1T[:, cols]).then_inc(m_filled[i], 1)
                if kind == "s2c":
                    i = take(pe, ring_m, m_freed, s)
                    for c in range(HC):
                        read(pe, ring_m, m_freed, ("enc", f, c))
                        last = mm(ps_m[i][M * c:M * c + M, cols], w_s2c[:, c, :], spikes[:, c, cols])
                    last.then_inc(m_filled[i], 1)
                if kind == "router":
                    i = take(pe, ring_m, m_freed, s)
                    read(pe, ring_m, m_freed, ("s2c", f))
                    for t in range(t0, t1):
                        last = mm(ps_m[i][:, E * t:E * t + E], cont[:, P * t:P * t + P], wr[:, :])
                    last.then_inc(m_filled[i], 1)
                if kind == "w1":
                    ring, ps, filled_, freed = home(s)
                    i = take(pe, ring, freed, s)
                    mm(ps[i][:, cols], w1[:, s[2], :], cont[:, cols]).then_inc(filled_[i], 1)
                if kind == "gateT":
                    i = take(pe, ring_m, m_freed, s)
                    pe.wait_ge(routed, ROUTE * (f + 1))
                    for t in range(t0, t1):
                        last = turn(ps_m[i][0:E, P * t:P * t + P], gate[:, t, :])
                    last.then_inc(m_filled[i], 1)
                if kind == "gate":
                    ring, ps, filled_, freed = home(s)
                    i = take(pe, ring, freed, s)
                    if s[2] == 0:
                        pe.wait_ge(gate_split, 4 * (f + 1))
                    mm(ps[i][:, cols], sel[:, s[2], :, :].rearrange("r i m -> r (i m)"), gs[:, cols]
                       ).then_inc(filled_[i], 1)
                if kind == "w2":
                    i = take(pe, ring_m, m_freed, s)
                    for n in range(2):
                        e = 2 * s[2] + n
                        hidden = ("w1", f, e)
                        read(pe, home(hidden)[0], home(hidden)[3], hidden)
                        last = mm(ps_m[i][M * n:M * n + M, cols], w2[:, e, :], hs[:, e, cols])
                    last.then_inc(m_filled[i], 1)
                if kind == "c2s":
                    i = take(pe, ring_m, m_freed, s)
                    pe.wait_ge(y_ready, f + 1)
                    mm(ps_m[i][:, cols], w_c2s[:, P * s[2]:P * s[2] + P], cont[:, cols]).then_inc(m_filled[i], 1)
                if kind == "dec":
                    i = take(pe, ring_m, m_freed, s)
                    for c in range(HC):
                        read(pe, ring_m, m_freed, ("c2s", f, c))
                    for t in range(t0, t1):
                        for c in range(HC):
                            last = mm(ps_m[i][:, P * t:P * t + P], spikes[:, c, P * t:P * t + P], w_dec[:, c, :],
                                      start=(c == 0), stop=(c == HC - 1))
                    last.then_inc(m_filled[i], 1)

        @block.vector
        def _(dve):
            def stats(src, st, mv, done, before, t0, t1):
                for t in range(t0, t1):
                    nc.vector.bn_stats(st[:, t, :], src[:, t, :]).then_inc(done, 1)
                for t in range(t0, t1):
                    dve.wait_ge(done, before + t1 - t0 + t - t0)
                    nc.vector.bn_aggr(mv[:, t, :], st[:, t, :]).then_inc(done, 1)

            def apply_norm(dst, src, mv, rs, done, t0, t1):
                for t in range(t0, t1):
                    nc.vector.tensor_scalar(dst[:, t, :], src[:, t, :], mv[:, t, 0:1], rs[:, t:t + 1],
                                            ALU.subtract, ALU.mult).then_inc(done, 1)

            def split2(f, p1, r, p2, p3, done, before):
                if before:
                    dve.wait_ge(done, before)
                nc.vector.tensor_tensor(r, f, p1, ALU.subtract).then_inc(done, 1)
                dve.wait_ge(done, before + 1)
                nc.vector.tensor_copy(p2, r).then_inc(done, 1)
                dve.wait_ge(done, before + 2)
                nc.vector.tensor_tensor(p3, r, p2, ALU.subtract).then_inc(done, 1)

            nc.vector.memset(ones[:, :], 1.0).then_inc(tiles_set, 1)
            nc.vector.memset(gs[:, :], 0.0).then_inc(tiles_set, 1)

            def route(f, part, t0, t1):
                base = ROUTE * f
                done = [(2, 7, 13)[part]]

                def wide(x):
                    return x[:, t0:t1].unsqueeze(2).to_broadcast([P, t1 - t0, E])

                def then(ins):
                    ins.then_inc(routed, 1)
                    done[0] += 1
                    dve.wait_ge(routed, base + done[0])

                def tt(dst, x, w, op):
                    then(nc.vector.tensor_tensor(dst[:, t0:t1, :], x[:, t0:t1, :], w, op))

                def reduce(src, op):
                    then(nc.vector.tensor_reduce(r1[:, t0:t1], src[:, t0:t1, :], AX_X, op))

                if part == 0:
                    dve.wait_ge(route_exp, f + 1)
                    reduce(ex, ALU.max)
                    tt(ra, ex, wide(r1), ALU.is_equal)
                    tt(ra, ra, tie_rank[:, t0:t1, :], ALU.mult)
                    reduce(ra, ALU.max)
                    tt(oh1, ra, wide(r1), ALU.is_equal)
                elif part == 1:
                    then(nc.vector.scalar_tensor_tensor(out=rb[:, t0:t1, :], in0=oh1[:, t0:t1, :], scalar=-2.0,
                                                        in1=ex[:, t0:t1, :], op0=ALU.mult, op1=ALU.add))
                    reduce(rb, ALU.max)
                    tt(ra, rb, wide(r1), ALU.is_equal)
                    tt(ra, ra, tie_rank[:, t0:t1, :], ALU.mult)
                    reduce(ra, ALU.max)
                    tt(oh2, ra, wide(r1), ALU.is_equal)
                else:
                    tt(oh1, oh1, oh2[:, t0:t1, :], ALU.add)
                    tt(ra, ex, oh1[:, t0:t1, :], ALU.mult)
                    reduce(ra, ALU.add)
                    then(nc.vector.reciprocal(r1[:, t0:t1], r1[:, t0:t1]))
                    tt(gate, ra, wide(r1), ALU.mult)

            for s in steps:
                kind = s[0]
                b, f, t0, t1 = span(s)
                tl, cols = slice(t0, t1), slice(P * t0, P * t1)
                xb = x_all[:, T * b + t0:T * b + t1, :]
                if kind == "stats1":
                    dve.wait_ge(x_in[b], 16)
                    if b:
                        dve.wait_ge(xn_ready, T * b)
                    stats(xb, st1, mv1, ln1, 2 * T * b, 0, T)
                if kind == "norm1":
                    dve.wait_ge(rstd1, 2 * (b + 1))
                    if b:
                        j, r = bank(ring_a, ("xT", b - 1))
                        dve.wait_ge(a_filled[j], r + 1)
                    apply_norm(xn, xb, mv1, rs1, xn_ready, 0, T)
                if kind == "norm1" and b == 0:
                    dve.wait_ge(bias_in, 16 * 2)
                    nc.vector.tensor_scalar(bqs[:, :], bq_raw[:, :], QSCALE, None, ALU.mult).then_inc(bqs_ready, 1)
                if kind in ("q", "k"):
                    w = int(kind == "k")
                    read(dve, ring_a, a_freed, s)
                    dve.wait_ge(qk_high, 2 * b + w + 1)
                    split2(qkf[:, w, :], parts[:, w, 0, :], qkr[:, :], parts[:, w, 1, :], parts[:, w, 2, :],
                           qk_split, SPLIT * b + 3 * w)
                if kind == "v":
                    i = full(dve, ring_a, a_filled, s)
                    if b == 0:
                        dve.wait_ge(vp_ones, 4)
                        dve.wait_ge(qkv_in, 16 * 3)
                    if b >= 2:
                        dve.wait_ge(pv_done, NSET * (b - 1))
                    for n in range(2):
                        heads = slice(GH * n, GH * n + GH)
                        src = ps_a[i][:, :].rearrange("p (a h k) -> p a h k", h=2 * GH, k=DK)[:, :, heads, :]
                        bias = bv[:, :, :].rearrange("p t (a h k) -> p (t a) h k", h=2 * GH, k=DK)[:, :, heads, :]
                        dst = vp[b % 2][:, :, :, :].rearrange("p t (a h) w -> p (t a) h w", h=2 * GH)
                        o = nc.vector.tensor_tensor(dst[:, :, heads, SLOT * n:SLOT * n + DK], src, bias, ALU.add)
                    o.then_inc(a_freed[i], 1)
                if kind == "ffn_setup":
                    dve.wait_ge(ffn_in, 16 * len(ffn_loads))
                    nc.vector.tensor_scalar(w_s2c[:, :, :], w_s2c[:, :, :], 0.5, None, ALU.mult).then_inc(halved, 1)
                    nc.vector.tensor_scalar(w_dec[:, :, :], w_dec[:, :, :], 0.5, None, ALU.mult).then_inc(halved, 1)
                    nc.vector.tensor_scalar(b_enc[:, :], b_enc[:, :], 0.5, None, ALU.mult).then_inc(halved, 1)
                    nc.vector.tensor_scalar(b_c2s[:, :], b_c2s[:, :], 0.5, None, ALU.mult).then_inc(halved, 1)
                    i = full(dve, ring_m, m_filled, s)
                    nc.vector.tensor_tensor(b_s2c[0:M, :], b_s2c[0:M, :], ps_m[i][0:M, 0:1], ALU.add)
                    nc.vector.tensor_tensor(b_dec[:, :], b_dec[:, :], ps_m[i][:, P:P + D], ALU.add
                                            ).then_inc(m_freed[i], 1)
                if kind == "max":
                    t, h0, nh = MU[s[2]]
                    i = full(dve, ring_a, a_filled, s)
                    W = P * (t + 1)
                    src = ps_a[i][:, 0:nh * W].rearrange("p (n w) -> p n w", n=nh)
                    nc.vector.tensor_reduce(mx[:, t, h0:h0 + nh], src, AX_X, ALU.max).then_inc(a_freed[i], 1)
                if kind == "negmax":
                    n = order_negmax[s]
                    c = slice(HQ * s[2], HQ * s[2] + HQ)
                    i = full(dve, ring_a, a_filled, s)
                    if b:
                        dve.wait_ge(nm_in[order_negmax[("negmax", b - 1, s[2])]], 16 * M_PARTS)
                    nc.vector.tensor_copy(nmp[:, 0, c], ps_a[i][0:H, 0:HQ]).then_inc(nm_split, 1)
                    dve.wait_ge(nm_split, n + 1)
                    nc.vector.tensor_tensor(nmp[:, 1, c], ps_a[i][0:H, 0:HQ], nmp[:, 0, c], ALU.subtract
                                            ).then_inc(a_freed[i], 1)
                if kind == "ctx_tok":
                    half = s[2]
                    i = full(dve, ring_m, m_filled, s)
                    v = ps_m[i][:, :].rearrange("p (t j c) -> p t j c", t=T, c=VW)
                    if b or half:
                        read(dve, ring_m, m_freed, ("ctx_tok", b - 1, 1) if half == 0 else ("ctx_tok", b, 0))
                    nc.vector.reciprocal(rsum[:, :, :, :], v[:, :, :, DK:DK + SLOT + 1:SLOT]).then_inc(recip, 1)
                    dve.wait_ge(recip, 2 * b + half + 1)
                    if half == 0 and b:
                        j, r = bank(ring_m, ("ctxT", b - 1))
                        dve.wait_ge(m_filled[j], r + 1)
                    dst = ctok[:, 2 * half:2 * half + 2, :].rearrange("p t (a n j k) -> p (t a) n j k", a=2, n=2, k=DK)
                    for n in range(2):
                        o = nc.vector.tensor_tensor(
                            dst[:, :, n], v[:, :, :, SLOT * n:SLOT * n + DK],
                            rsum[:, :, :, n:n + 1].to_broadcast([P, T, GH, DK]), ALU.mult)
                    o.then_inc(m_freed[i], 1)
                if kind == "out_proj":
                    i = full(dve, ring_m, m_filled, s)
                    dve.wait_ge(x_bo, b + 1)
                    if f and t0 == 0:
                        dve.wait_ge(x1_lnb, f)
                    nc.vector.tensor_tensor(x1[:, tl, :], ps_m[i][:, cols].rearrange("p (t d) -> p t d", d=D),
                                            xb, ALU.add).then_inc(m_freed[i], 1)
                if kind == "stats2":
                    read(dve, ring_m, m_freed, ("out_proj", f))
                    if f and t0 == 0:
                        dve.wait_ge(xn2_ready, tiles_before[f])
                    stats(x1, st2, mv2, ln2, 2 * tiles_before[f], t0, t1)
                if kind == "norm2":
                    if f and t0 == 0:
                        full(dve, ring_m, m_filled, ("x1T", f - 1))
                    dve.wait_ge(rstd2, 2 * (f + 1))
                    apply_norm(xn2, x1, mv2, rs2, xn2_ready, t0, t1)
                if kind == "router":
                    i = full(dve, ring_m, m_filled, s)
                    nc.vector.tensor_tensor(lg[:, tl, :],
                                            ps_m[i][:, E * t0:E * t1].rearrange("p (t e) -> p t e", e=E),
                                            br[:, tl, :], ALU.add).then_inc(m_freed[i], 1)
                    read(dve, ring_m, m_freed, s)
                    nc.vector.tensor_reduce(r1[:, tl], lg[:, tl, :], AX_X, ALU.max).then_inc(routed, 1)
                    dve.wait_ge(routed, ROUTE * f + 1)
                    nc.vector.tensor_tensor(lg[:, tl, :], lg[:, tl, :],
                                            r1[:, tl].unsqueeze(2).to_broadcast([P, t1 - t0, E]), ALU.subtract
                                            ).then_inc(routed, 1)
                if kind == "route":
                    if s[2] == 0:
                        dve.wait_ge(routed, ROUTE * f + 2)
                    route(f, s[2], t0, t1)
                if kind == "gateT":
                    read(dve, ring_m, m_freed, s)
                    dve.wait_ge(gate_high, f + 1)
                    split2(gf[:, cols], gs[0:E, cols], gr[:, cols], g2[:, cols], gs[64:64 + E, cols],
                           gate_split, 4 * f)
                    nc.vector.tensor_copy(gs[32:32 + E, cols], g2[:, cols]).then_inc(gate_split, 1)
                if kind == "w2":
                    p_ = s[2]
                    if p_ == E // 2 - 1:
                        read(dve, ring_m, m_freed, ("w2", f, p_ - 1))
                        dve.wait_ge(w2_pool, f + 1)
                        nc.vector.tensor_tensor(gb[:, 2, cols], gb[:, 0, cols], gb[:, 2, cols], ALU.add
                                                ).then_inc(w2_sum, 1)
                    i = full(dve, ring_m, m_filled, s)
                    spread = ("gate", f, p_)
                    read(dve, home(spread)[0], home(spread)[3], spread)
                    nc.vector.scalar_tensor_tensor(out=gb[:, p_, cols], in0=ps_m[i][:, cols],
                                                   scalar=b2[:, p_:p_ + 1], in1=gb[:, p_, cols],
                                                   op0=ALU.add, op1=ALU.mult).then_inc(m_freed[i], 1)
                    if p_ == E // 2 - 1:
                        read(dve, ring_m, m_freed, s)
                        dve.wait_ge(w2_sum, f + 1)
                        nc.vector.tensor_tensor(cont[:, cols], gb[:, 2, cols], gb[:, 3, cols], ALU.add
                                                ).then_inc(y_ready, 1)
                if kind == "dec":
                    i = full(dve, ring_m, m_filled, s)
                    if f and t0 == 0:
                        dve.wait_ge(stored, 16 * f)
                    nc.vector.tensor_tensor(z[:, tl, :], ps_m[i][:, cols].rearrange("p (t d) -> p t d", d=D),
                                            b_dec[:, :].unsqueeze(1).to_broadcast([P, t1 - t0, D]), ALU.add
                                            ).then_inc(m_freed[i], 1)
                    read(dve, ring_m, m_freed, s)
                    if f and t0 == 0:
                        dve.wait_ge(zn_ready, tiles_before[f])
                    stats(z, st3, mv3, ln3, 2 * tiles_before[f], t0, t1)
                if kind == "norm3":
                    dve.wait_ge(rstd3, 2 * (f + 1))
                    apply_norm(z, z, mv3, rs3, zn_ready, t0, t1)
                if kind == "result":
                    dve.wait_ge(zn_scaled, f + 1)
                    dve.wait_ge(x1_lnb, f + 1)
                    nc.vector.tensor_tensor(z[:, tl, :], z[:, tl, :], xb, ALU.add).then_inc(res_ready, 1)


_INS = ["L0_attn_embeddings", "L0_attn_Wq", "L0_attn_bq", "L0_attn_Wk", "L0_attn_bk", "L0_attn_Wv", "L0_attn_bv",
        "L0_attn_Wo", "L0_attn_bo", "L0_ffn_W_enc", "L0_ffn_b_enc", "L0_ffn_W_s2c", "L0_ffn_b_s2c", "L0_ffn_Wr",
        "L0_ffn_br", "L0_ffn_W1", "L0_ffn_b1", "L0_ffn_W2", "L0_ffn_b2", "L0_ffn_W_c2s", "L0_ffn_b_c2s",
        "L0_ffn_W_dec", "L0_ffn_b_dec", "L0_ffn_ln_g", "L0_ffn_ln_b"]


def kernel(**inputs):
    import numpy as np
    from concourse import bacc
    from concourse.bass_utils import run_bass_kernel_spmd

    nc = bacc.Bacc("TRN2", target_bir_lowering=False, num_devices=1)
    arrays, aps = {}, {}
    for name in _INS:
        arrays[f"in_{name}"] = np.ascontiguousarray(inputs[name])
        aps[name] = nc.dram_tensor(f"in_{name}", arrays[f"in_{name}"].shape, F32, kind="ExternalInput").ap()
    out = nc.dram_tensor("out", arrays["in_L0_attn_embeddings"].shape, F32, kind="ExternalOutput").ap()
    build(nc, aps, out)
    return run_bass_kernel_spmd(nc, [arrays], core_ids=[0]).results[0]["out"]
```
